# Optimizing a Trainium2 kernel written in Bass

```python
import numpy as np
import jax
import jax.numpy as jnp

def _softmax(x, axis=-1):
    return jax.nn.softmax(x, axis=axis)

def _gelu(x):
    return jax.nn.gelu(x, approximate=True)

def _silu(x):
    return jax.nn.silu(x)

def _sigmoid(x):
    return jax.nn.sigmoid(x)

def _layernorm(x, axis=-1, eps=1e-05):
    m = jnp.mean(x, axis=axis, keepdims=True)
    v = jnp.var(x, axis=axis, keepdims=True)
    return (x - m) / jnp.sqrt(v + eps)

def _scatter_add(tgt, idx, src, axis=0):
    return tgt.at[idx].add(src)

def _segment_sum(src, seg, n):
    return jax.ops.segment_sum(src, seg, n)
kernel_name = 'mk_vit_tower_cls_d1_tok_img1024_r4_6b4f64'

def setup_inputs(seed: int=0):
    np.random.seed(seed)
    _w = jnp.asarray

    def _rec_inputs():
        import jax
        import jax.numpy as jnp
        _rk = jax.random.key(seed)
        x = -0.00016672 + 0.999947 * jax.random.normal(jax.random.fold_in(_rk, 1), (16, 3, 96, 96), jnp.float32)
        cls_tok = 0.02 * jax.random.normal(jax.random.fold_in(_rk, 5), (1, 1, 256), jnp.float32)
        return (x, cls_tok)
    x, cls_tok = _rec_inputs()

    def _L0_tok_setup():
        import jax, jax.numpy as jnp
        import numpy as np
        EMBED_DIM = 256
        IMAGE_SIZE = 96
        CHANNELS = 3
        PATCH = 16
        NUM_PATCHES = (IMAGE_SIZE // PATCH) ** 2
        PATCH_DIM = PATCH * PATCH * CHANNELS

        def _patchify(x, patch):
            B, C, H, W = x.shape
            hp, wp = (H // patch, W // patch)
            x = x.reshape(B, C, hp, patch, wp, patch)
            x = x.transpose(0, 2, 4, 1, 3, 5)
            return x.reshape(B, hp * wp, C * patch * patch)
        key = jax.random.key(seed)
        k_x, k_w, k_b, k_cls, k_pos = jax.random.split(key, 5)
        x = jax.random.normal(k_x, (64, CHANNELS, IMAGE_SIZE, IMAGE_SIZE), dtype=jnp.float32)
        W = jax.random.normal(k_w, (EMBED_DIM, PATCH_DIM), dtype=jnp.float32) / np.sqrt(PATCH_DIM)
        b = jax.random.normal(k_b, (EMBED_DIM,), dtype=jnp.float32) * 0.01
        cls_token = jax.random.normal(k_cls, (1, 1, EMBED_DIM), dtype=jnp.float32)
        pos_embedding = jax.random.normal(k_pos, (1, 1 + NUM_PATCHES, EMBED_DIM), dtype=jnp.float32)
        return {'x': x, 'W': W, 'b': b, 'cls_token': cls_token, 'pos_embedding': pos_embedding}
    _L0_tok_all = _L0_tok_setup()
    _L0_tok_in = {k: v for k, v in _L0_tok_all.items() if k in ('W', 'b', 'cls_token', 'pos_embedding')}
    del _L0_tok_all

    def _L0_attn_setup():
        import jax, jax.numpy as jnp
        import numpy as np
        D_MODEL = 256
        HEADS = 16
        SCALE = float(np.sqrt(D_MODEL / HEADS))
        key = jax.random.key(seed)
        ks = jax.random.split(key, 5)
        B, S, D = (4, 512, D_MODEL)
        q = jax.random.normal(ks[0], (B, S, D), dtype=jnp.float32)
        init = 0.02
        wq = jax.random.normal(ks[1], (D, D), dtype=jnp.float32) * init
        wk = jax.random.normal(ks[2], (D, D), dtype=jnp.float32) * init
        wv = jax.random.normal(ks[3], (D, D), dtype=jnp.float32) * init
        wo = jax.random.normal(ks[4], (D, D), dtype=jnp.float32) * init
        return {'q': q, 'wq': wq, 'wk': wk, 'wv': wv, 'wo': wo}
    _L0_attn_all = _L0_attn_setup()
    _L0_attn_in = {k: v for k, v in _L0_attn_all.items() if k in ('wq', 'wk', 'wv', 'wo')}
    del _L0_attn_all

    def _L0_ffn_setup():
        import jax, jax.numpy as jnp
        import numpy as np
        LORA_DIM = 16
        LORA_TOKEN_INDEX = 1
        B, S, D, H = (4, 512, 256, 1024)
        key = jax.random.key(seed)
        ks = jax.random.split(key, 6)
        x = jax.random.normal(ks[0], (B, S, D), dtype=jnp.float32)
        W1 = jax.random.normal(ks[1], (H, D), dtype=jnp.float32) * 0.02
        b1 = jnp.zeros((H,), dtype=jnp.float32)
        W2 = jax.random.normal(ks[2], (D, H), dtype=jnp.float32) * 0.02
        b2 = jnp.zeros((D,), dtype=jnp.float32)
        scale = jnp.asarray(0.001, dtype=jnp.float32)
        return {'x': x, 'W1': W1, 'b1': b1, 'W2': W2, 'b2': b2, 'scale': scale}
    _L0_ffn_all = _L0_ffn_setup()
    _L0_ffn_in = {k: v for k, v in _L0_ffn_all.items() if k in ('W1', 'b1', 'W2', 'b2', 'scale')}
    del _L0_ffn_all
    return {'x': x, 'cls_tok': cls_tok, 'L0_tok_W': _L0_tok_in['W'], 'L0_tok_b': _L0_tok_in['b'], 'L0_tok_cls_token': _L0_tok_in['cls_token'], 'L0_tok_pos_embedding': _L0_tok_in['pos_embedding'], 'L0_attn_wq': _L0_attn_in['wq'], 'L0_attn_wk': _L0_attn_in['wk'], 'L0_attn_wv': _L0_attn_in['wv'], 'L0_attn_wo': _L0_attn_in['wo'], 'L0_ffn_W1': _L0_ffn_in['W1'], 'L0_ffn_b1': _L0_ffn_in['b1'], 'L0_ffn_W2': _L0_ffn_in['W2'], 'L0_ffn_b2': _L0_ffn_in['b2'], 'L0_ffn_scale': _L0_ffn_in['scale']}

def reference(x, cls_tok, L0_tok_W, L0_tok_b, L0_tok_cls_token, L0_tok_pos_embedding, L0_attn_wq, L0_attn_wk, L0_attn_wv, L0_attn_wo, L0_ffn_W1, L0_ffn_b1, L0_ffn_W2, L0_ffn_b2, L0_ffn_scale):
    import jax
    import jax.numpy as jnp

    def _L0_tok_ref(x, W, b, cls_token, pos_embedding):
        import jax, jax.numpy as jnp
        import numpy as np
        EMBED_DIM = 256
        IMAGE_SIZE = 96
        CHANNELS = 3
        PATCH = 16
        NUM_PATCHES = (IMAGE_SIZE // PATCH) ** 2
        PATCH_DIM = PATCH * PATCH * CHANNELS

        def _patchify(x, patch):
            B, C, H, W = x.shape
            hp, wp = (H // patch, W // patch)
            x = x.reshape(B, C, hp, patch, wp, patch)
            x = x.transpose(0, 2, 4, 1, 3, 5)
            return x.reshape(B, hp * wp, C * patch * patch)
        B = x.shape[0]
        patches = _patchify(x, PATCH)
        tokens = jnp.einsum('bnd,ed->bne', patches, W) + b
        cls = jnp.broadcast_to(cls_token, (B, 1, EMBED_DIM))
        out = jnp.concatenate([cls, tokens], axis=1)
        return out + pos_embedding

    def _L0_attn_ref(q, wq, wk, wv, wo):
        import jax, jax.numpy as jnp
        import numpy as np
        D_MODEL = 256
        HEADS = 16
        SCALE = float(np.sqrt(D_MODEL / HEADS))
        B, S, D = q.shape
        Q = jnp.einsum('bsd,ed->bse', q, wq)
        K = jnp.einsum('bsd,ed->bse', q, wk)
        V = jnp.einsum('bsd,ed->bse', q, wv)
        scores = jnp.einsum('bqe,bke->bqk', Q, K) / SCALE
        attn = jax.nn.softmax(scores, axis=-1)
        out = jnp.einsum('bqk,bke->bqe', attn, V)
        out = jnp.transpose(out, (0, 2, 1)).reshape(B, S, D)
        return jnp.einsum('bsd,ed->bse', out, wo)

    def _L0_ffn_ref(x, W1, b1, W2, b2, scale):
        import jax, jax.numpy as jnp
        import numpy as np
        LORA_DIM = 16
        LORA_TOKEN_INDEX = 1
        B, S, D, H = (4, 512, 256, 1024)
        Bx, Sx, Dx = x.shape
        Hx = W1.shape[0]
        lt = jax.lax.dynamic_slice_in_dim(x, LORA_TOKEN_INDEX, LORA_DIM, axis=1)
        even = lt[:, ::2, :]
        odd = lt[:, 1::2, :]
        m1 = (even[:, :4, :, None] * odd[:, :4, None, :]).reshape(Bx, Hx, Dx)
        m2 = (even[:, 4:, :, None] * odd[:, 4:, None, :]).reshape(Bx, Dx, Hx)
        h = jnp.einsum('bsd,hd->bsh', x, W1) + scale * jnp.einsum('bsd,bhd->bsh', x, m1) + b1
        h = jax.nn.gelu(h, approximate=False)
        out = jnp.einsum('bsh,oh->bso', h, W2) + scale * jnp.einsum('bsh,boh->bso', h, m2) + b2
        return out
    h = _L0_tok_ref(x, L0_tok_W, L0_tok_b, L0_tok_cls_token, L0_tok_pos_embedding)
    h = jnp.concatenate([jnp.broadcast_to(cls_tok, (h.shape[0], 1, h.shape[2])), h], axis=1)
    h = h + _L0_attn_ref(_layernorm(h, axis=-1), L0_attn_wq, L0_attn_wk, L0_attn_wv, L0_attn_wo)
    h = h + _L0_ffn_ref(_layernorm(h, axis=-1), L0_ffn_W1, L0_ffn_b1, L0_ffn_W2, L0_ffn_b2, L0_ffn_scale)
    return h

_drawn_inputs = setup_inputs


def setup_inputs(seed=0):
    import zlib

    import numpy as np

    out = dict(_drawn_inputs(seed))
    spreads = {'L0_ffn_b1': (0.0, 0.31), 'L0_ffn_b2': (0.0, 0.1)}
    factors = {'cls_tok': 5.616,
     'L0_tok_b': 7.953,
     'L0_attn_wq': 8.0,
     'L0_attn_wk': 8.0,
     'L0_attn_wv': 3.715,
     'L0_attn_wo': 3.812}
    for name, (base, spread) in spreads.items():
        noise = np.random.default_rng([zlib.crc32(name.encode()), seed]).standard_normal(out[name].shape)
        drawn = base * np.exp(spread * noise) if base else spread * noise
        out[name] = jnp.asarray(drawn.astype(out[name].dtype))
    for name, factor in factors.items():
        out[name] = (out[name] * factor).astype(out[name].dtype)
    return out
```

```python
from contextlib import ExitStack

import numpy as np

import concourse.bass as bass
from concourse import mybir

F32 = mybir.dt.float32
F32R = mybir.dt.float32r
ALU = mybir.AluOpType
ACT = mybir.ActivationFunctionType

P = 128
B, CH, IMG, PATCH = 16, 3, 96, 16
NPATCH = (IMG // PATCH) ** 2
S = NPATCH + 2
D = 256
KD = CH * PATCH * PATCH
HID = 1024
EPS = 1e-5
KC, DC, HC = KD // P, D // P, HID // P
HALVES = 2
HB = B // HALVES
HT = HB * S
GROUP_IMAGES = (3, 3, 2)
GH = len(GROUP_IMAGES)
NG = HALVES * GH
GT = max(GROUP_IMAGES) * S
RANK = 4
PIECES = 3
PK = KC // PIECES
NROWS = 3 + 1 + NPATCH
LO_ROWS = 64
BANK = 512
OFF_BLOCK = 1e30

C_ID = 0
C_ATT = C_ID + P
C_PM = C_ATT + 3
C_GM = C_PM + HB
C_IM = C_GM + HB
C_SE = C_IM + RANK
C_SP = C_SE + 1
C_IND = C_SP + 1
NCONST = C_IND + GT


def constants():
    c = np.zeros((P, NCONST), np.float32)
    c[:, C_ID:C_ID + P] = np.eye(P)
    tok = np.arange(GT) // S
    c[:GT, C_ATT:C_ATT + 3] = np.where(tok[:, None] == np.arange(3)[None], 0.0, OFF_BLOCK)
    p = np.arange(P)
    b, r = p % HB, (p // HB) % 4
    own = (b[:, None] == np.arange(HB)[None]).astype(np.float32)
    c[:, C_PM:C_PM + HB] = own * np.array([1.0, -1.0, -1.0, 1.0])[r][:, None]
    c[:, C_GM:C_GM + HB] = own
    c[:, C_IM:C_IM + RANK] = ((p // HB) % RANK)[:, None] == np.arange(RANK)[None]
    c[:, C_SE] = r >= 2
    c[:, C_SP] = r % 2
    for t in range(GT):
        s = t % S
        for row in ([0] if s == 0 else [1, 3] if s == 1 else [2, 2 + s]):
            c[row, C_IND + t] = 1.0
            c[LO_ROWS + row, C_IND + t] = 1.0
    return c


def images_of(g):
    return sum(GROUP_IMAGES[:g % GH]), GROUP_IMAGES[g % GH]


def span(g):
    b0, nb = images_of(g)
    return slice(b0 * S, (b0 + nb) * S), nb * S


def build(nc, x_t, w_t, rows, consts, wq, wk, wv_t, wo_t, w1_t, w2_t, b1_t, b2_t, scale, out_t):
    ctx = ExitStack()
    with ctx:
        def sb(name, shape, dt=F32):
            return ctx.enter_context(nc.sbuf_tensor(name, shape, dt))

        def sem(name):
            return ctx.enter_context(nc.semaphore(name))

        scratch = nc.dram_tensor("scratch", [B, D, S], F32, kind="Internal").ap()

        xr = sb("xr", [P, HALVES, KC, HT])
        x_hi = sb("x_hi", [P, HALVES, KC, HT], F32R)
        x_lo = sb("x_lo", [P, HALVES, KC, HT], F32R)
        w = sb("w", [P, KC, D])
        w_hi = sb("w_hi", [P, KC, D], F32R)
        w_lo = sb("w_lo", [P, KC, D], F32R)
        add_rows = sb("add_rows", [LO_ROWS + NROWS, D])
        add_hl = sb("add_hl", [LO_ROWS + NROWS, D], F32R)
        ind = sb("ind", [LO_ROWS + NROWS, GT], F32R)
        con = sb("con", [P, NCONST])
        wq_sb = sb("wq_sb", [P, DC, D])
        wk_sb = sb("wk_sb", [P, DC, D])
        wv_sb = sb("wv_sb", [P, DC, D])
        wo_sb = sb("wo_sb", [P, DC, D])
        w1 = sb("w1", [P, DC, HID])
        w1_hi = sb("w1_hi", [P, DC, HID], F32R)
        w1_lo = sb("w1_lo", [P, DC, HID], F32R)
        w2 = sb("w2", [P, HC, D])
        w2_hi = sb("w2_hi", [P, HC, D], F32R)
        w2_lo = sb("w2_lo", [P, HC, D], F32R)
        b1_sb = sb("b1_sb", [P, HC])
        b2_sb = sb("b2_sb", [P, DC])
        scale_sb = sb("scale_sb", [P, 1])
        warm = sb("warm", [1, 2])
        expo = sb("expo", [GT, GH])
        h = sb("h", [GT, NG, D])
        xn = sb("xn", [GT, NG, D])
        stats = sb("stats", [GT, 4, GH, 6])
        mv = sb("mv", [GT, 4, GH, 2])
        ve = sb("ve", [GT, 4, GH])
        rstd = sb("rstd", [GT, 4, GH])
        amat = sb("amat", [P, DC, D])
        xT = sb("xT", [P, HALVES, DC, HT])
        tT = sb("tT", [P, HALVES, DC, HT])
        v = sb("v", [GT, NG, D])
        sc = sb("sc", [GT, NG, GT])
        pr = sb("pr", [GT, NG, GT])
        negmax = sb("negmax", [GT, NG])
        rsum = sb("rsum", [GT, NG])
        rinv = sb("rinv", [GT, NG])
        pT = sb("pT", [GT, NG, GT])
        oT = sb("oT", [P, NG, DC, GT])
        o2 = v
        o2T = sb("o2T", [P, HALVES, DC, HT])
        h2 = sb("h2", [GT, NG, D])
        h2T = xT
        x2T = w[:, :, :].rearrange("p k d -> p (k d)")[:, 0:HALVES * DC * HT].rearrange(
            "p (h c t) -> p h c t", h=HALVES, c=DC)
        x2_hi = sb("x2_hi", [P, HALVES, DC, HT], F32R)
        x2_lo = sb("x2_lo", [P, HALVES, DC, HT], F32R)
        pscaled = sb("pscaled", [P, HT])
        p_hi = sb("p_hi", [P, HT], F32R)
        p_part = sb("p_part", [P, HT])
        pm = sb("pm", [P, HALVES, HT], F32R)
        ev_raw = sb("ev_raw", [P, D])
        ev_hi = sb("ev_hi", [P, D], F32R)
        ev = sb("ev", [P, HALVES, D], F32R)
        e4 = sb("e4", [P, HALVES, D])
        gm = sb("gm", [P, HALVES, HT])
        even1 = sb("even1", [P, DC, P])
        odd1_hi = sb("odd1_hi", [P, DC, P], F32R)
        odd1_lo = sb("odd1_lo", [P, DC, P], F32R)
        even2 = sb("even2", [P, HALVES, DC, P])
        odd2 = sb("odd2", [P, HALVES, DC, RANK * HB])
        outT = tT
        gr = xr[:, :, :, :].rearrange("p h k t -> p (h k t)")[:, 0:HC * HT].rearrange("p (k t) -> p k t", k=HC)
        g_hi = x_hi[:, :, :, :].rearrange("p h k t -> p (h k t)")[:, 0:HC * HT].rearrange("p (k t) -> p k t", k=HC)
        g_lo = x_lo[:, :, :, :].rearrange("p h k t -> p (h k t)")[:, 0:HC * HT].rearrange("p (k t) -> p k t", k=HC)

        bank = [ctx.enter_context(nc.psum_tensor(f"bank{i}", [P, BANK], F32)) for i in range(8)]

        def tok_bank(g):
            return bank[g % GH]

        def v_bank(g):
            return bank[(7, 1, 2)[g % GH]]

        def score_bank(g):
            return bank[3 + g % GH]

        def pT_bank(g):
            return bank[6 + g % 2]

        def row_bank(g):
            return bank[g % 2]

        def o2T_bank(half, c):
            return bank[((6, 2), (7, 2))[half][c]]

        ld_w = [sem(f"ld_tok_w{i}") for i in range(PIECES)]
        ld_x = [sem(f"ld_x{i}") for i in range(HALVES * PIECES)]
        ld_rows, ld_con, ld_qk, ld_wv, ld_wo = sem("ld_rows"), sem("ld_con"), sem("ld_qk"), sem("ld_wv"), sem("ld_wo")
        ld_w1, ld_w2, ld_vec = sem("ld_hid_w"), sem("ld_out_w"), sem("ld_vec")
        st_o = [sem(f"st_o{g}") for g in range(NG)]
        ld_o = [sem(f"ld_o{g}") for g in range(NG)]
        st_out = sem("st_out")
        whi_done, wlo_done, xhi_done, xlo_done = sem("whi_done"), sem("wlo_done"), sem("xhi_done"), sem("xlo_done")
        rows_done, w1hi_done, w1lo_done, w2hi_done, w2lo_done = (
            sem("rows_done"), sem("w1hi_done"), sem("w1lo_done"), sem("w2hi_done"), sem("w2lo_done"))
        pe_tok, pe_amat, pe_xT, pe_T, pe_v, pe_s, pe_pT, pe_oT, pe_o2T, pe_y = (
            sem(n) for n in ("pe_tok", "pe_amat", "pe_xT", "pe_T", "pe_v", "pe_s", "pe_pT", "pe_oT", "pe_o2T", "pe_y"))
        pe_x2T, pe_h2T, pe_p, pe_ev, pe_e4, pe_f1, pe_g, pe_f2 = (
            sem(n) for n in ("pe_x2T", "pe_h2T", "pe_p", "pe_ev", "pe_e4", "pe_f1", "pe_g", "pe_f2"))
        h_ready, var_ready, rstd_ready, xn_ready, amat_ready, xT_ready, tT_ready, v_ready = (
            sem(n) for n in ("h_ready", "var_ready", "rstd_ready", "xn_ready", "amat_ready", "xT_ready",
                             "tT_ready", "v_ready"))
        sc_ready, exp_ready, pr_ready, pT_ready, oT_ready, o2T_ready, h2_ready = (
            sem(n) for n in ("sc_ready", "exp_ready", "pr_ready", "pT_ready", "oT_ready", "o2T_ready", "h2_ready"))
        x2T_ready, x2s_ready, h2T_ready, pscaled_ready, pm_ready, ev_ready, odd1_hi_ready, odd1_lo_ready, even1_ready, even2_ready, odd2_ready, e4_ready, gelu_ready, gs_ready, gm_ready, out_ready = (
            sem(n) for n in ("x2T_ready", "x2s_ready", "h2T_ready", "pscaled_ready", "pm_ready", "ev_ready",
                             "odd1_hi_ready", "odd1_lo_ready", "even1_ready", "even2_ready", "odd2_ready", "e4_ready",
                             "gelu_ready", "gs_ready", "gm_ready", "out_ready"))
        init_done, mv_init, dve_chain = sem("init_done"), sem("mv_init"), sem("dve_chain")

        def factors(half, first, c):
            return x2T[:, half, c, :].rearrange("p (b s) -> p s b", s=S)[:, first:first + 2 * RANK - 1:2, :]

        def inner(t):
            return t.unsqueeze(2).to_broadcast([P, RANK, 4, HB])

        def outer(t):
            return t.unsqueeze(1).to_broadcast([P, RANK, RANK, HB])

        def four(t):
            return t.rearrange("p (i r b) -> p i r b", i=RANK, b=HB)

        block = ctx.enter_context(nc.Block())

        @block.sync
        def _(sync):
            sync.dma_start(add_rows[0:NROWS, :], rows).then_inc(ld_rows, 16)
            sync.dma_start(add_rows[LO_ROWS:LO_ROWS + NROWS, :], rows).then_inc(ld_rows, 16)
            for i in range(PIECES):
                k = slice(PK * i, PK * (i + 1))
                sync.dma_start(w[:, k, :], w_t[:, k, :]).then_inc(ld_w[i], 16)
                sync.dma_start(xr[:, 0, k, :], x_t[0, :, k, :]).then_inc(ld_x[i], 16)
                if i == 0:
                    sync.dma_start(con[:, :], consts).then_inc(ld_con, 16)
            sync.dma_start(wq_sb[:, :, :], wq).then_inc(ld_qk, 16)
            sync.dma_start(wk_sb[:, :, :], wk).then_inc(ld_qk, 16)
            for i in range(PIECES):
                k = slice(PK * i, PK * (i + 1))
                sync.dma_start(xr[:, 1, k, :], x_t[1, :, k, :]).then_inc(ld_x[PIECES + i], 16)
            sync.dma_start(wv_sb[:, :, :], wv_t).then_inc(ld_wv, 16)
            sync.dma_start(w1[:, :, :], w1_t).then_inc(ld_w1, 16)
            sync.dma_start(wo_sb[:, :, :], wo_t).then_inc(ld_wo, 16)
            sync.dma_start(w2[:, :, :], w2_t).then_inc(ld_w2, 16)
            sync.dma_start(b1_sb[:, :], b1_t).then_inc(ld_vec, 16)
            sync.dma_start(b2_sb[:, :], b2_t).then_inc(ld_vec, 16)
            sync.dma_start(scale_sb[:, :], scale.to_broadcast([P, 1])).then_inc(ld_vec, 16)
            for g in range(NG):
                b0, nb = images_of(g)
                b0 += HB * (g // GH)
                sync.wait_ge(st_o[g], 16 * DC)
                sync.dma_start(o2[0:nb * S, g, :],
                               scratch[b0:b0 + nb, :, :].rearrange("b e q -> (b e q)")
                               .rearrange("(r d) -> r d", d=D)).then_inc(ld_o[g], 16)
            for half in range(HALVES):
                for c in range(DC):
                    sync.wait_ge(out_ready, half * DC + c + 1)
                    sync.dma_start(out_t[c, :, half * HT:(half + 1) * HT], outT[:, half, c, :]).then_inc(st_out, 16)
            sync.wait_ge(st_out, 16 * HALVES * DC)

        @block.gpsimd
        def _(pool):
            nc.gpsimd.memset(expo[:, :], -0.5).then_inc(init_done, 1)
            nc.gpsimd.memset(mv[:, :, :, :], 1.0).then_inc(mv_init, 1)
            pool.wait_ge(init_done, 1)

            def powers(n):
                pool.wait_ge(var_ready, n + 1)
                nc.gpsimd.tensor_tensor(rstd[:, n, :], ve[:, n, :], expo[:, :], ALU.pow).then_inc(rstd_ready, 1)

            powers(0)
            for c in range(DC):
                pool.wait_ge(w1hi_done, c + 1)
                nc.gpsimd.tensor_tensor(w1_lo[:, c, :], w1[:, c, :], w1_hi[:, c, :], ALU.subtract).then_inc(w1lo_done, 1)
            powers(1)
            for c in range(4):
                k = slice(2 * c, 2 * c + 2)
                pool.wait_ge(w2hi_done, c // 2 + 1)
                nc.gpsimd.tensor_tensor(w2_lo[:, k, :], w2[:, k, :], w2_hi[:, k, :], ALU.subtract).then_inc(w2lo_done, 1)
                if c == 1:
                    powers(2)

            def second_factors(half):
                pool.wait_ge(x2T_ready, DC * (half + 1))
                for c in range(DC):
                    nc.gpsimd.tensor_copy(four(even2[:, half, c, :]), outer(factors(half, 9, c))).then_inc(even2_ready, 1)
                for c in range(DC):
                    nc.gpsimd.tensor_copy(odd2[:, half, c, :].rearrange("p (i b) -> p i b", i=RANK),
                                          factors(half, 10, c)).then_inc(odd2_ready, 1)

            second_factors(0)
            powers(3)
            second_factors(1)

        @block.scalar
        def _(act):
            act.wait_ge(init_done, 1)
            nc.scalar.activation(warm[0:1, 0:1], expo[0:1, 0:1], ACT.Exp)

            def x_high(i):
                act.wait_ge(ld_x[i], 16)
                half, k = i // PIECES, slice(PK * (i % PIECES), PK * (i % PIECES + 1))
                nc.scalar.copy(x_hi[:, half, k, :], xr[:, half, k, :]).then_inc(xhi_done, 1)

            def w_high(i):
                act.wait_ge(ld_w[i], 16)
                k = slice(PK * i, PK * (i + 1))
                nc.scalar.copy(w_hi[:, k, :], w[:, k, :]).then_inc(whi_done, 1)

            def h_rows(g):
                n = span(g)[1]
                act.wait_ge(pe_tok, g + 1)
                nc.scalar.copy(h[0:n, g, :], tok_bank(g)[0:n, 0:D]).then_inc(h_ready, 1)

            def move_xT(half):
                for c in range(DC):
                    act.wait_ge(pe_xT, DC * half + c + 1)
                    nc.scalar.copy(xT[:, half, c, :], bank[3 + c][:, 0:HT]).then_inc(xT_ready, 1)

            def move_v(g):
                n = span(g)[1]
                act.wait_ge(pe_v, g + 1)
                nc.scalar.copy(v[0:n, g, :], v_bank(g)[0:n, 0:D]).then_inc(v_ready, 1)

            def exps(g):
                n = span(g)[1]
                act.wait_ge(sc_ready, g + 1)
                nc.scalar.activation(pr[0:n, g, 0:n], sc[0:n, g, 0:n], ACT.Exp, bias=negmax[0:n, g:g + 1],
                                     scale=-1.0, accum_out=rsum[0:n, g:g + 1]).then_inc(exp_ready, 1)

            def move_oT(g):
                b0, nb = images_of(g)
                b0 += HB * (g // GH)
                n = nb * S
                act.wait_ge(pe_oT, g + 1)
                nc.scalar.copy(oT[:, g, :, 0:n], row_bank(g)[:, 0:DC * n].rearrange("p (c t) -> p c t", c=DC))\
                    .then_inc(oT_ready, 1)
                act.wait_ge(oT_ready, g + 1)
                for c in range(DC):
                    act.dma_start(scratch[b0:b0 + nb, P * c:P * (c + 1), :].rearrange("b e q -> e b q"),
                                  oT[:, g, c, 0:n].rearrange("p (b q) -> p b q", q=S)).then_inc(st_o[g], 16)

            def move_o2T(half):
                for c in range(DC):
                    act.wait_ge(pe_o2T, DC * half + c + 1)
                    nc.scalar.copy(o2T[:, half, c, :], o2T_bank(half, c)[:, 0:HT]).then_inc(o2T_ready, 1)

            def move_x2T(half):
                for c in range(DC):
                    act.wait_ge(pe_x2T, DC * half + c + 1)
                    nc.scalar.copy(x2T[:, half, c, :], bank[3 + c][:, 0:HT]).then_inc(x2T_ready, 1)

            def first_factors(half):
                act.wait_ge(x2T_ready, DC * (half + 1))
                if half:
                    act.wait_ge(pe_p, half)
                    act.wait_ge(pe_ev, half)
                for c in range(DC):
                    nc.scalar.copy(four(odd1_hi[:, c, :]), inner(factors(half, 2, c))).then_inc(odd1_hi_ready, 1)
                for c in range(DC):
                    nc.scalar.copy(four(even1[:, c, :]), inner(factors(half, 1, c))).then_inc(even1_ready, 1)

            def move_h2T(half):
                for c in range(DC):
                    act.wait_ge(pe_h2T, DC * half + c + 1)
                    nc.scalar.copy(h2T[:, half, c, :], bank[5 + c][:, 0:HT]).then_inc(h2T_ready, 1)

            def scaled(half):
                act.wait_ge(pe_p, half + 1)
                if half:
                    act.wait_ge(pm_ready, half)
                nc.scalar.mul(pscaled[:, :], bank[7][:, 0:HT], scale_sb[:, 0:1]).then_inc(pscaled_ready, 1)

            def gelus(half, ks):
                for k in ks:
                    act.wait_ge(pe_f1, HC * half + k + 1)
                    if half:
                        act.wait_ge(pe_g, 1)
                    nc.scalar.activation(gr[:, k, :], bank[3 + k % 4][:, 0:HT], ACT.Gelu,
                                         bias=b1_sb[:, k:k + 1]).then_inc(gelu_ready, 1)

            for i in range(PIECES):
                w_high(i)
                x_high(i)
            for i in range(PIECES, 2 * PIECES):
                x_high(i)
            for g in range(GH + 1):
                h_rows(g)
            move_xT(0)
            for g in range(GH):
                move_v(g)
            for g in range(GH):
                exps(g)
            h_rows(4)
            h_rows(5)
            act.wait_ge(ld_w1, 16)
            for c in range(DC):
                nc.scalar.copy(w1_hi[:, c, :], w1[:, c, :]).then_inc(w1hi_done, 1)
            for g in range(GH):
                move_oT(g)
            move_xT(1)
            for g in range(GH, NG):
                move_v(g)
            for g in range(GH, NG):
                exps(g)
            act.wait_ge(ld_w2, 16)
            for c in range(2):
                k = slice(4 * c, 4 * c + 4)
                nc.scalar.copy(w2_hi[:, k, :], w2[:, k, :]).then_inc(w2hi_done, 1)
            move_o2T(0)
            for g in range(GH, NG):
                move_oT(g)
            act.wait_ge(ld_vec, 48)
            nc.scalar.activation(warm[0:1, 1:2], expo[0:1, 0:1], ACT.Gelu)
            move_x2T(0)
            first_factors(0)
            move_h2T(0)
            scaled(0)
            gelus(0, range(4))
            move_o2T(1)
            gelus(0, range(4, HC))
            move_x2T(1)
            first_factors(1)
            move_h2T(1)
            scaled(1)
            gelus(1, range(HC))

        @block.vector
        def _(dve):
            chained = [0]

            def then(instruction):
                chained[0] += 1
                instruction.then_inc(dve_chain, 1)
                dve.wait_ge(dve_chain, chained[0])

            def w_low(i):
                k = slice(PK * i, PK * (i + 1))
                dve.wait_ge(ld_w[i], 16)
                dve.wait_ge(whi_done, i + 1)
                nc.vector.tensor_tensor(w_lo[:, k, :], w[:, k, :], w_hi[:, k, :], ALU.subtract).then_inc(wlo_done, 1)

            def x_low(i):
                half, k = i // PIECES, slice(PK * (i % PIECES), PK * (i % PIECES + 1))
                dve.wait_ge(ld_x[i], 16)
                dve.wait_ge(xhi_done, i + 1)
                nc.vector.tensor_tensor(x_lo[:, half, k, :], xr[:, half, k, :], x_hi[:, half, k, :],
                                        ALU.subtract).then_inc(xlo_done, 1)

            def norm_stats(n, rows_, ready, g):
                t, i = span(g)[1], g % GH
                dve.wait_ge(ready, g + 1)
                then(nc.vector.bn_stats(stats[0:t, n, i, :], rows_[0:t, g, :]))
                nc.vector.bn_aggr(mv[0:t, n, i, :], stats[0:t, n, i, :]).then_inc(dve_chain, 1)
                chained[0] += 1

            def norm_var(n):
                dve.wait_ge(dve_chain, chained[0])
                nc.vector.tensor_scalar(ve[:, n, :], mv[:, n, :, 1], EPS, None, ALU.add).then_inc(var_ready, 1)

            def norm_rows(n, rows_, g):
                t, i = span(g)[1], g % GH
                dve.wait_ge(rstd_ready, n + 1)
                if n >= HALVES:
                    dve.wait_ge(pe_xT, DC * (n - 1))
                nc.vector.tensor_scalar(xn[0:t, g, :], rows_[0:t, g, :], mv[0:t, n, i, 0:1], rstd[0:t, n, i:i + 1],
                                        ALU.subtract, ALU.mult).then_inc(xn_ready, 1)

            def move_T(half):
                for c in range(DC):
                    dve.wait_ge(pe_T, DC * half + c + 1)
                    nc.vector.tensor_copy(tT[:, half, c, :], bank[5 + c][:, 0:HT]).then_inc(tT_ready, 1)

            def masked_max(g):
                nb = images_of(g)[1]
                n = nb * S
                dve.wait_ge(pe_s, g + 1)
                nc.vector.tensor_tensor_reduce(
                    out=sc[0:n, g, 0:n].rearrange("p (b k) -> p b k", k=S),
                    in0=score_bank(g)[0:n, 0:n].rearrange("p (b k) -> p b k", k=S),
                    in1=con[0:n, C_ATT:C_ATT + nb].unsqueeze(2).to_broadcast([n, nb, S]),
                    scale=1.0, scalar=3e38, op0=ALU.add, op1=ALU.min,
                    accum_out=negmax[0:n, g:g + 1]).then_inc(sc_ready, 1)

            def softmax_end(g):
                n = span(g)[1]
                dve.wait_ge(exp_ready, g + 1)
                then(nc.vector.reciprocal(rinv[0:n, g:g + 1], rsum[0:n, g:g + 1]))
                nc.vector.tensor_scalar(pr[0:n, g, 0:n], pr[0:n, g, 0:n], rinv[0:n, g:g + 1], None,
                                        ALU.mult).then_inc(pr_ready, 1)

            def move_pT(g):
                n = span(g)[1]
                dve.wait_ge(pe_pT, g + 1)
                nc.vector.tensor_copy(pT[0:n, g, 0:n], pT_bank(g)[0:n, 0:n]).then_inc(pT_ready, 1)

            def residual(g):
                n = span(g)[1]
                dve.wait_ge(pe_y, g + 1)
                nc.vector.tensor_tensor(h2[0:n, g, :], row_bank(g)[0:n, 0:D], h[0:n, g, :], ALU.add)\
                    .then_inc(h2_ready, 1)

            def split_x2(half):
                for c in range(DC):
                    dve.wait_ge(x2T_ready, DC * half + c + 1)
                    then(nc.vector.tensor_copy(x2_hi[:, half, c, :], x2T[:, half, c, :]))
                    nc.vector.tensor_tensor(x2_lo[:, half, c, :], x2T[:, half, c, :], x2_hi[:, half, c, :],
                                            ALU.subtract).then_inc(x2s_ready, 1)

            def odd_low(half):
                for c in range(DC):
                    dve.wait_ge(odd1_hi_ready, DC * half + c + 1)
                    nc.vector.tensor_tensor(four(odd1_lo[:, c, :]), inner(factors(half, 2, c)),
                                            four(odd1_hi[:, c, :]), ALU.subtract).then_inc(odd1_lo_ready, 1)

            def factors_ready(half):
                dve.wait_ge(pe_ev, half + 1)
                then(nc.vector.tensor_copy(ev_raw[:, :], bank[2][:, 0:D]))
                then(nc.vector.tensor_copy(ev_hi[:, :], ev_raw[:, :]))
                nc.vector.scalar_tensor_tensor(out=ev[:, half, :], in0=ev_raw[:, :],
                                               scalar=con[:, C_SE:C_SE + 1], in1=ev_hi[:, :],
                                               op0=ALU.mult, op1=ALU.subtract).then_inc(ev_ready, 1)

            def second_even(half):
                dve.wait_ge(pe_e4, half + 1)
                for j in range(RANK):
                    rows_ = slice(32 * j, 32 * (j + 1))
                    last = nc.vector.tensor_tensor(
                        e4[rows_, half, :].rearrange("p (i o) -> p i o", i=RANK),
                        bank[2][rows_, j:D:RANK].unsqueeze(1).to_broadcast([32, RANK, D // RANK]),
                        con[rows_, C_IM:C_IM + RANK].unsqueeze(2).to_broadcast([32, RANK, D // RANK]), ALU.mult)
                last.then_inc(e4_ready, 1)

            def projection_parts(half):
                dve.wait_ge(pscaled_ready, half + 1)
                then(nc.vector.tensor_copy(p_hi[:, :], pscaled[:, :]))
                then(nc.vector.scalar_tensor_tensor(out=p_part[:, :], in0=pscaled[:, :],
                                                    scalar=con[:, C_SP:C_SP + 1], in1=p_hi[:, :],
                                                    op0=ALU.mult, op1=ALU.subtract))
                nc.vector.tensor_tensor(
                    pm[:, half, :].rearrange("p (b s) -> p b s", s=S),
                    p_part[:, :].rearrange("p (b s) -> p b s", s=S),
                    con[:, C_PM:C_PM + HB].unsqueeze(2).to_broadcast([P, HB, S]), ALU.mult).then_inc(pm_ready, 1)

            def split_g(half, ks):
                for k in ks:
                    dve.wait_ge(gelu_ready, HC * half + k + 1)
                    if half:
                        dve.wait_ge(pe_f2, DC)
                    then(nc.vector.tensor_copy(g_hi[:, k, :], gr[:, k, :]))
                    nc.vector.tensor_tensor(g_lo[:, k, :], gr[:, k, :], g_hi[:, k, :], ALU.subtract)\
                        .then_inc(gs_ready, 1)

            def mask_g(half):
                dve.wait_ge(pe_g, half + 1)
                nc.vector.scalar_tensor_tensor(
                    out=gm[:, half, :].rearrange("p (b s) -> p b s", s=S),
                    in0=bank[7][:, 0:HT].rearrange("p (b s) -> p b s", s=S), scalar=scale_sb[:, 0:1],
                    in1=con[:, C_GM:C_GM + HB].unsqueeze(2).to_broadcast([P, HB, S]),
                    op0=ALU.mult, op1=ALU.mult).then_inc(gm_ready, 1)

            def finish(half):
                for c in range(DC):
                    dve.wait_ge(pe_f2, DC * half + c + 1)
                    dve.wait_ge(h2T_ready, DC * half + c + 1)
                    nc.vector.scalar_tensor_tensor(out=outT[:, half, c, :], in0=bank[c][:, 0:HT],
                                                   scalar=b2_sb[:, c:c + 1], in1=h2T[:, half, c, :],
                                                   op0=ALU.add, op1=ALU.add).then_inc(out_ready, 1)

            w_low(0)
            x_low(0)
            dve.wait_ge(ld_rows, 32)
            dve.wait_ge(ld_con, 16)
            nc.vector.tensor_copy(ind[:, :], con[0:LO_ROWS + NROWS, C_IND:C_IND + GT])
            then(nc.vector.memset(add_hl[:, :].bitcast(F32), 0.0))
            then(nc.vector.tensor_copy(add_hl[0:NROWS, :], add_rows[0:NROWS, :]))
            then(nc.vector.tensor_copy(add_hl[LO_ROWS:LO_ROWS + NROWS, :], add_rows[LO_ROWS:LO_ROWS + NROWS, :]))
            nc.vector.tensor_tensor(add_hl[LO_ROWS:LO_ROWS + NROWS, :], add_rows[LO_ROWS:LO_ROWS + NROWS, :],
                                    add_hl[LO_ROWS:LO_ROWS + NROWS, :], ALU.subtract).then_inc(rows_done, 1)
            for i in range(1, PIECES):
                w_low(i)
                x_low(i)
            for i in range(PIECES, 2 * PIECES):
                x_low(i)
            dve.wait_ge(pe_amat, 1)
            nc.vector.tensor_scalar(amat[:, :, :].rearrange("p c d -> p (c d)"), bank[5][:, :], -0.25, None,
                                    ALU.mult).then_inc(amat_ready, 1)
            dve.wait_ge(mv_init, 1)
            for g in range(GH):
                norm_stats(0, h, h_ready, g)
            norm_var(0)
            for g in range(GH):
                norm_rows(0, h, g)
            norm_stats(1, h, h_ready, 3)
            move_T(0)
            for g in range(GH):
                masked_max(g)
            for g in range(GH):
                softmax_end(g)
            for g in range(4, NG):
                norm_stats(1, h, h_ready, g)
            norm_var(1)
            for g in range(GH):
                move_pT(g)
            for g in range(GH, NG):
                norm_rows(1, h, g)
            move_T(1)
            for g in range(GH, NG):
                masked_max(g)
            for g in range(GH, NG):
                softmax_end(g)
            for g in range(GH):
                residual(g)
                norm_stats(2, h2, h2_ready, g)
            norm_var(2)
            for g in range(GH, NG):
                move_pT(g)
            for g in range(GH):
                norm_rows(2, h2, g)
            dve.wait_ge(ld_vec, 48)
            split_x2(0)
            odd_low(0)
            factors_ready(0)
            projection_parts(0)
            split_g(0, range(4))
            for g in range(GH, NG):
                residual(g)
                norm_stats(3, h2, h2_ready, g)
            norm_var(3)
            split_g(0, range(4, 6))
            for g in range(GH, NG):
                norm_rows(3, h2, g)
            split_g(0, range(6, HC))
            split_x2(1)
            odd_low(1)
            factors_ready(1)
            projection_parts(1)
            second_even(0)
            mask_g(0)
            finish(0)
            split_g(1, range(HC))
            second_even(1)
            mask_g(1)
            finish(1)

        @block.tensor
        def _(pe):
            ident = con[:, C_ID:C_ID + P]

            def three(out, s_hi, s_lo, m_hi, m_lo, start, stop):
                nc.tensor.matmul(out, s_lo, m_hi, start=start, stop=False)
                nc.tensor.matmul(out, s_hi, m_lo, start=False, stop=False)
                return nc.tensor.matmul(out, s_hi, m_hi, start=False, stop=stop)

            def tok_piece(g, i):
                half, (cols, n) = g // GH, span(g)
                for k in range(PK * i, PK * (i + 1)):
                    three(tok_bank(g)[0:n, 0:D], x_hi[:, half, k, cols], x_lo[:, half, k, cols],
                          w_hi[:, k, :], w_lo[:, k, :], k == 0, False)

            def tok_rows(g):
                n = span(g)[1]
                pe.wait_ge(rows_done, 1)
                nc.tensor.matmul(tok_bank(g)[0:n, 0:D], ind[:, 0:n], add_hl[:, :], start=False, stop=True)\
                    .then_inc(pe_tok, 1)

            def tok_group(g):
                pe.wait_ge(h_ready, g - GH + 1)
                if g > GH:
                    pe.wait_ge(v_ready, g - GH + 1)
                pe.wait_ge(xhi_done, 2 * PIECES)
                pe.wait_ge(xlo_done, 2 * PIECES)
                for i in range(PIECES):
                    tok_piece(g, i)
                tok_rows(g)

            def to_T(rows_, half, c, out, done):
                for g in range(half * GH, (half + 1) * GH):
                    cols, n = span(g)
                    last = nc.tensor.transpose(out[:, cols], rows_[0:n, g, P * c:P * (c + 1)], ident[0:n, 0:n])
                last.then_inc(done, 1)

            def x_T(half):
                pe.wait_ge(xn_ready, GH * (half + 1))
                if half:
                    pe.wait_ge(sc_ready, 2)
                for c in range(DC):
                    to_T(xn, half, c, bank[3 + c], pe_xT)

            def t_T(half):
                pe.wait_ge(amat_ready, 1)
                pe.wait_ge(xT_ready, DC * (half + 1))
                if half:
                    pe.wait_ge(sc_ready, GH)
                    pe.wait_ge(pT_ready, GH)
                for c in range(DC):
                    for k in range(DC):
                        last = nc.tensor.matmul(bank[5 + c][:, 0:HT], amat[:, k, P * c:P * (c + 1)],
                                                xT[:, half, k, :], start=k == 0, stop=k == DC - 1)
                    last.then_inc(pe_T, 1)

            def values(g):
                half, (cols, n) = g // GH, span(g)
                pe.wait_ge(ld_wv, 16)
                if half:
                    pe.wait_ge(oT_ready, GH)
                    pe.wait_ge(h_ready, NG)
                for k in range(DC):
                    last = nc.tensor.matmul(v_bank(g)[0:n, 0:D], xT[:, half, k, cols], wv_sb[:, k, :],
                                            start=k == 0, stop=k == DC - 1)
                last.then_inc(pe_v, 1)

            def scores(g):
                half, (cols, n) = g // GH, span(g)
                pe.wait_ge(tT_ready, DC * (half + 1))
                for k in range(DC):
                    last = nc.tensor.matmul(score_bank(g)[0:n, 0:n], tT[:, half, k, cols], xT[:, half, k, cols],
                                            start=k == 0, stop=k == DC - 1)
                last.then_inc(pe_s, 1)

            def attend_T(g):
                n = span(g)[1]
                pe.wait_ge(pr_ready, g + 1)
                if g >= 2:
                    pe.wait_ge(pT_ready, g - 1)
                nc.tensor.transpose(pT_bank(g)[0:n, 0:n], pr[0:n, g, 0:n], ident[0:n, 0:n]).then_inc(pe_pT, 1)

            def attend(g):
                n = span(g)[1]
                pe.wait_ge(pT_ready, g + 1)
                pe.wait_ge(v_ready, g + 1)
                if g < GH:
                    pe.wait_ge(h_ready, 5 if g == 1 else 4)
                    if g == 2:
                        pe.wait_ge(oT_ready, 1)
                else:
                    pe.wait_ge(h2_ready, GH)
                    if g == NG - 1:
                        pe.wait_ge(oT_ready, 4)
                for c in range(DC):
                    last = nc.tensor.matmul(row_bank(g)[:, c * n:(c + 1) * n], v[0:n, g, P * c:P * (c + 1)],
                                            pT[0:n, g, 0:n], start=True, stop=True)
                last.then_inc(pe_oT, 1)

            def o2_T(half):
                if half == 0:
                    pe.wait_ge(tT_ready, 2 * DC)
                    pe.wait_ge(v_ready, NG)
                else:
                    pe.wait_ge(pscaled_ready, 1)
                    pe.wait_ge(ev_ready, 1)
                for g in range(half * GH, (half + 1) * GH):
                    pe.wait_ge(ld_o[g], 16)
                for c in range(DC):
                    to_T(o2, half, c, o2T_bank(half, c), pe_o2T)

            def project(g):
                half, (cols, n) = g // GH, span(g)
                pe.wait_ge(ld_wo, 16)
                pe.wait_ge(o2T_ready, DC * (half + 1))
                if g < GH:
                    pe.wait_ge(oT_ready, GH)
                    if g == 2:
                        pe.wait_ge(h2_ready, 1)
                else:
                    pe.wait_ge(oT_ready, NG)
                    if g == NG - 1:
                        pe.wait_ge(h2_ready, 4)
                for k in range(DC):
                    last = nc.tensor.matmul(row_bank(g)[0:n, 0:D], o2T[:, half, k, cols], wo_sb[:, k, :],
                                            start=k == 0, stop=k == DC - 1)
                last.then_inc(pe_y, 1)

            def second_T(half):
                pe.wait_ge(xn_ready, GH * (HALVES + half + 1))
                if half == 0:
                    pe.wait_ge(sc_ready, NG)
                    pe.wait_ge(pT_ready, NG)
                else:
                    pe.wait_ge(gelu_ready, HC)
                for c in range(DC):
                    to_T(xn, half, c, bank[3 + c], pe_x2T)
                for c in range(DC):
                    to_T(h2, half, c, bank[5 + c], pe_h2T)

            def low_rank(half):
                pe.wait_ge(even1_ready, DC * (half + 1))
                pe.wait_ge(o2T_ready, DC * (half + 1))
                for c in range(DC):
                    last = nc.tensor.transpose(bank[2][:, P * c:P * (c + 1)], even1[:, c, :], ident)
                last.then_inc(pe_ev, 1)
                pe.wait_ge(x2s_ready, DC * (half + 1))
                pe.wait_ge(odd1_lo_ready, DC * (half + 1))
                for c in range(DC):
                    last = three(bank[7][:, 0:HT], odd1_hi[:, c, :], odd1_lo[:, c, :], x2_hi[:, half, c, :],
                                 x2_lo[:, half, c, :], c == 0, c == DC - 1)
                last.then_inc(pe_p, 1)

            def second_even_rows(half):
                pe.wait_ge(even2_ready, DC * (half + 1))
                pe.wait_ge(ev_ready, HALVES)
                for c in range(DC):
                    last = nc.tensor.transpose(bank[2][:, P * c:P * (c + 1)], even2[:, half, c, :], ident)
                last.then_inc(pe_e4, 1)

            def hidden(half, ks):
                pe.wait_ge(w1lo_done, DC)
                pe.wait_ge(h2T_ready, DC * (half + 1))
                for k in ks:
                    if k >= 4:
                        pe.wait_ge(gelu_ready, HC * half + k - 3)
                    out = bank[3 + k % 4][:, 0:HT]
                    cols = slice(P * k, P * (k + 1))
                    for c in range(DC):
                        three(out, w1_hi[:, c, cols], w1_lo[:, c, cols], x2_hi[:, half, c, :], x2_lo[:, half, c, :],
                              c == 0, False)
                    i, c = k // 2, k % 2
                    pe.wait_ge(pm_ready, half + 1)
                    pe.wait_ge(ev_ready, half + 1)
                    nc.tensor.matmul(out, ev[32 * i:32 * (i + 1), half, P * c:P * (c + 1)],
                                     pm[32 * i:32 * (i + 1), half, :], start=False, stop=True).then_inc(pe_f1, 1)

            def output(half, ks):
                if half == 0:
                    pe.wait_ge(h2_ready, NG)
                else:
                    pe.wait_ge(out_ready, DC)
                for k in ks:
                    pe.wait_ge(w2lo_done, k // 2 + 1)
                    pe.wait_ge(gs_ready, HC * half + k + 1)
                    for c in range(DC):
                        cols = slice(P * c, P * (c + 1))
                        three(bank[c][:, 0:HT], w2_hi[:, k, cols], w2_lo[:, k, cols], g_hi[:, k, :], g_lo[:, k, :],
                              k == 0, False)

            def hidden_on_odd(half):
                pe.wait_ge(gelu_ready, HC * (half + 1))
                pe.wait_ge(odd2_ready, DC * (half + 1))
                pe.wait_ge(pscaled_ready, HALVES)
                for c in range(DC):
                    for j in range(RANK):
                        last = nc.tensor.matmul(bank[7][32 * j:32 * (j + 1), 0:HT], odd2[:, half, c, :],
                                                gr[:, DC * j + c, :], start=c == 0, stop=c == DC - 1)
                last.then_inc(pe_g, 1)

            def output_low_rank(half):
                pe.wait_ge(gm_ready, half + 1)
                pe.wait_ge(e4_ready, half + 1)
                for c in range(DC):
                    nc.tensor.matmul(bank[c][:, 0:HT], e4[:, half, P * c:P * (c + 1)], gm[:, half, :],
                                     start=False, stop=True).then_inc(pe_f2, 1)

            for i in range(PIECES):
                pe.wait_ge(whi_done, i + 1)
                pe.wait_ge(wlo_done, i + 1)
                pe.wait_ge(xhi_done, i + 1)
                pe.wait_ge(xlo_done, i + 1)
                for g in range(GH):
                    tok_piece(g, i)
            for g in range(GH):
                tok_rows(g)
            pe.wait_ge(ld_qk, 32)
            pe.wait_ge(ld_con, 16)
            for c in range(DC):
                for k in range(DC):
                    last = nc.tensor.matmul(bank[5][:, D * c:D * (c + 1)], wq_sb[:, k, P * c:P * (c + 1)],
                                            wk_sb[:, k, :], start=k == 0, stop=k == DC - 1)
            last.then_inc(pe_amat, 1)
            tok_group(3)
            x_T(0)
            t_T(0)
            for g in range(GH):
                values(g)
            for g in range(GH):
                scores(g)
            tok_group(4)
            tok_group(5)
            for g in range(GH):
                attend_T(g)
                attend(g)
            x_T(1)
            t_T(1)
            for g in range(GH, NG):
                values(g)
            for g in range(GH, NG):
                scores(g)
            o2_T(0)
            for g in range(GH):
                project(g)
            for g in range(GH, NG):
                attend_T(g)
                attend(g)
            second_T(0)
            low_rank(0)
            hidden(0, range(4))
            o2_T(1)
            for g in range(GH, NG):
                project(g)
            hidden(0, range(4, HC))
            second_T(1)
            low_rank(1)
            output(0, range(HC))
            second_even_rows(0)
            hidden_on_odd(0)
            output_low_rank(0)
            hidden(1, range(HC))
            output(1, range(6))
            second_even_rows(1)
            hidden_on_odd(1)
            output(1, range(6, HC))
            output_low_rank(1)


def kernel(x, cls_tok, L0_tok_W, L0_tok_b, L0_tok_cls_token, L0_tok_pos_embedding, L0_attn_wq, L0_attn_wk,
           L0_attn_wv, L0_attn_wo, L0_ffn_W1, L0_ffn_b1, L0_ffn_W2, L0_ffn_b2, L0_ffn_scale):
    import concourse.bacc as bacc
    from concourse.bass_utils import run_bass_kernel_spmd

    def chunks(a):
        a = np.asarray(a)
        return np.ascontiguousarray(a.reshape(-1, P, a.shape[1]).transpose(1, 0, 2))

    n = IMG // PATCH
    patches = np.asarray(x).reshape(B, CH, n, PATCH, n, PATCH).transpose(0, 2, 4, 1, 3, 5).reshape(B, NPATCH, KD)
    tokens = np.zeros((B, S, KD), np.float32)
    tokens[:, S - NPATCH:, :] = patches
    x_t = tokens.reshape(HALVES, HT, KC, P).transpose(0, 3, 2, 1)
    rows = np.concatenate([np.asarray(cls_tok).reshape(1, D), np.asarray(L0_tok_cls_token).reshape(1, D),
                           np.asarray(L0_tok_b).reshape(1, D), np.asarray(L0_tok_pos_embedding).reshape(-1, D)])
    arrays = {
        "x_t": x_t, "w_t": chunks(np.asarray(L0_tok_W).T), "rows": rows, "consts": constants(),
        "wq": chunks(L0_attn_wq), "wk": chunks(L0_attn_wk),
        "wv_t": chunks(np.asarray(L0_attn_wv).T), "wo_t": chunks(np.asarray(L0_attn_wo).T),
        "w1_t": chunks(np.asarray(L0_ffn_W1).T), "w2_t": chunks(np.asarray(L0_ffn_W2).T),
        "b1_t": np.asarray(L0_ffn_b1).reshape(HC, P).T, "b2_t": np.asarray(L0_ffn_b2).reshape(DC, P).T,
        "scale": np.asarray(L0_ffn_scale).reshape(1, 1),
    }
    arrays = {k: np.ascontiguousarray(a) for k, a in arrays.items()}
    nc = bacc.Bacc("TRN2", target_bir_lowering=False, num_devices=1)
    args = [nc.dram_tensor(k, a.shape, mybir.dt.from_np(a.dtype), kind="ExternalInput").ap() for k, a in arrays.items()]
    out_t = nc.dram_tensor("out_t", (DC, P, B * S), F32, kind="ExternalOutput").ap()
    build(nc, *args, out_t)
    result = run_bass_kernel_spmd(nc, [arrays], core_ids=[0]).results[0]["out_t"]
    return np.ascontiguousarray(result.reshape(D, B, S).transpose(1, 2, 0))
```

```python
from contextlib import ExitStack

import numpy as np

import concourse.bass as bass
from concourse import mybir

F32 = mybir.dt.float32
F32R = mybir.dt.float32r
ALU = mybir.AluOpType
ACT = mybir.ActivationFunctionType

P = 128
B, CH, IMG, PATCH = 16, 3, 96, 16
NPATCH = (IMG // PATCH) ** 2
S = NPATCH + 2
D = 256
KD = CH * PATCH * PATCH
HID = 1024
EPS = 1e-5
KC, DC, HC = KD // P, D // P, HID // P
HALVES = 2
HB = B // HALVES
HT = HB * S
GROUP_IMAGES = (3, 3, 2)
GH = len(GROUP_IMAGES)
NG = HALVES * GH
GT = max(GROUP_IMAGES) * S
OB = 4
OR = HT // OB
RANK = 4
PIECES = 3
PK = KC // PIECES
NROWS = 3 + 1 + NPATCH
LO_ROWS = 64
BANK = 512
WARM = 10
OFF_BLOCK = 1e30

C_ID = 0
C_ATT = C_ID + P
C_PM = C_ATT + 3
C_GM = C_PM + HB
C_IM = C_GM + HB
C_SE = C_IM + RANK
C_SP = C_SE + 1
C_IND = C_SP + 1
NCONST = C_IND + GT


def constants():
    c = np.zeros((P, NCONST), np.float32)
    c[:, C_ID:C_ID + P] = np.eye(P)
    tok = np.arange(GT) // S
    c[:GT, C_ATT:C_ATT + 3] = np.where(tok[:, None] == np.arange(3)[None], 0.0, OFF_BLOCK)
    p = np.arange(P)
    b, r = p % HB, (p // HB) % 4
    own = (b[:, None] == np.arange(HB)[None]).astype(np.float32)
    c[:, C_PM:C_PM + HB] = own * np.array([1.0, -1.0, -1.0, 1.0])[r][:, None]
    c[:, C_GM:C_GM + HB] = own
    c[:, C_IM:C_IM + RANK] = ((p // HB) % RANK)[:, None] == np.arange(RANK)[None]
    c[:, C_SE] = r >= 2
    c[:, C_SP] = r % 2
    for t in range(GT):
        s = t % S
        for row in ([0] if s == 0 else [1, 3] if s == 1 else [2, 2 + s]):
            c[row, C_IND + t] = 1.0
            c[LO_ROWS + row, C_IND + t] = 1.0
    return c


def images_of(g):
    return sum(GROUP_IMAGES[:g % GH]), GROUP_IMAGES[g % GH]


def span(g):
    b0, nb = images_of(g)
    return slice(b0 * S, (b0 + nb) * S), nb * S


def build(nc, x_t, w_t, rows, consts, wq, wk, wv_t, wo_t, w1_t, w2_t, b1_t, b2_t, scale, out_t):
    ctx = ExitStack()
    with ctx:
        def sb(name, shape, dt=F32):
            return ctx.enter_context(nc.sbuf_tensor(name, shape, dt))

        def sem(name):
            return ctx.enter_context(nc.semaphore(name))

        scratch = nc.dram_tensor("scratch", [B, D, S], F32, kind="Internal").ap()

        xr = sb("xr", [P, HALVES, KC, HT])
        x_hi = sb("x_hi", [P, HALVES, KC, HT], F32R)
        x_lo = sb("x_lo", [P, HALVES, KC, HT], F32R)
        w = sb("w", [P, KC, D])
        w_hi = sb("w_hi", [P, KC, D], F32R)
        w_lo = sb("w_lo", [P, KC, D], F32R)
        add_rows = sb("add_rows", [LO_ROWS + NROWS, D])
        add_hl = sb("add_hl", [LO_ROWS + NROWS, D], F32R)
        ind = sb("ind", [LO_ROWS + NROWS, GT], F32R)
        con = sb("con", [P, NCONST])
        wq_sb = sb("wq_sb", [P, DC, D])
        wk_sb = sb("wk_sb", [P, DC, D])
        wv_sb = sb("wv_sb", [P, DC, D])
        wo_sb = sb("wo_sb", [P, DC, D])
        w1 = sb("w1", [P, DC, HID])
        w1_hi = sb("w1_hi", [P, DC, HID], F32R)
        w1_lo = sb("w1_lo", [P, DC, HID], F32R)
        w2 = sb("w2", [P, HC, D])
        w2_hi = sb("w2_hi", [P, HC, D], F32R)
        w2_lo = sb("w2_lo", [P, HC, D], F32R)
        b1_sb = sb("b1_sb", [P, HC])
        b2_sb = sb("b2_sb", [P, DC])
        scale_sb = sb("scale_sb", [P, 1])
        warm = sb("warm", [1, 2])
        warm_in = sb("warm_in", [P, P])
        expo = sb("expo", [GT, GH])
        h = sb("h", [GT, NG, D])
        xn = sb("xn", [GT, NG, D])
        stats = sb("stats", [GT, 4, GH, 6])
        mv = sb("mv", [GT, 4, GH, 2])
        ve = sb("ve", [GT, 4, GH])
        rstd = sb("rstd", [GT, 4, GH])
        amat = sb("amat", [P, DC, D])
        xT = sb("xT", [P, HALVES, DC, HT])
        tT = sb("tT", [P, HALVES, DC, HT])
        v = sb("v", [GT, NG, D])
        sc = sb("sc", [GT, NG, GT])
        pr = sb("pr", [GT, NG, GT])
        negmax = sb("negmax", [GT, NG])
        rsum = sb("rsum", [GT, NG])
        rinv = sb("rinv", [GT, NG])
        pT = sb("pT", [GT, NG, GT])
        oT = sb("oT", [P, NG, DC, GT])
        o2T = sb("o2T", [P, HALVES, DC, HT])
        h2 = sb("h2", [GT, NG, D])
        h2T = xT
        x2T = w[:, :, :].rearrange("p k d -> p (k d)")[:, 0:HALVES * DC * HT].rearrange(
            "p (h c t) -> p h c t", h=HALVES, c=DC)
        x2_hi = sb("x2_hi", [P, HALVES, DC, HT], F32R)
        x2_lo = sb("x2_lo", [P, HALVES, DC, HT], F32R)
        pscaled = sb("pscaled", [P, HT])
        p_hi = sb("p_hi", [P, HT], F32R)
        p_part = sb("p_part", [P, HT])
        pm = sb("pm", [P, HALVES, HT], F32R)
        ev_raw = sb("ev_raw", [P, D])
        ev_hi = sb("ev_hi", [P, D], F32R)
        ev = sb("ev", [P, HALVES, D], F32R)
        e4 = sb("e4", [P, HALVES, D])
        gm = sb("gm", [P, HALVES, HT])
        even1 = sb("even1", [P, DC, P])
        odd1_hi = sb("odd1_hi", [P, DC, P], F32R)
        odd1_lo = sb("odd1_lo", [P, DC, P], F32R)
        even2 = sb("even2", [P, HALVES, DC, P])
        odd2 = sb("odd2", [P, HALVES, DC, RANK * HB])
        outT = tT
        xr_flat = xr[:, :, :, :].rearrange("p h k t -> p (h k t)")
        o2 = [xr_flat[0:OR, at:at + OB * D].rearrange("p (o d) -> p o d", o=OB) for at in (HC * HT, 0)]
        gr = xr[:, :, :, :].rearrange("p h k t -> p (h k t)")[:, 0:HC * HT].rearrange("p (k t) -> p k t", k=HC)
        g_hi = x_hi[:, :, :, :].rearrange("p h k t -> p (h k t)")[:, 0:HC * HT].rearrange("p (k t) -> p k t", k=HC)
        g_lo = x_lo[:, :, :, :].rearrange("p h k t -> p (h k t)")[:, 0:HC * HT].rearrange("p (k t) -> p k t", k=HC)

        bank = [ctx.enter_context(nc.psum_tensor(f"bank{i}", [P, BANK], F32)) for i in range(8)]

        def tok_bank(g):
            return bank[g % GH]

        def xT_bank(half, c):
            return bank[((3, 4), (2, 6))[half][c]]

        def t_bank(half, c):
            return bank[((5, 6), (7, 0))[half][c]]

        def v_bank(g):
            return bank[(7, 0, 1, 5, 4, 5)[g]]

        def score_bank(g):
            return bank[(3, 4, 5, 0, 1, 3)[g]]

        def pT_bank(g):
            return bank[(1, 3, 4, 2, 6, 7)[g]]

        def oT_bank(g):
            return bank[(2, 6, 7, 0, 1, 3)[g]]

        def o2T_bank(half, c):
            return bank[((4, 5), (0, 1))[half][c]]

        def y_bank(g):
            return bank[(2, 6, 7, 3, 4, 5)[g]]

        def hid_bank(k):
            return bank[(1, 3, 4, 5)[k % 4]]

        end_bank = (bank[2], bank[6])
        even_bank, odd_bank = bank[0], bank[7]

        ld_w = [sem(f"ld_tok_w{i}") for i in range(PIECES)]
        ld_x = [sem(f"ld_x{i}") for i in range(HALVES * PIECES)]
        ld_rows, ld_con, ld_qk, ld_wv, ld_wo = sem("ld_rows"), sem("ld_con"), sem("ld_qk"), sem("ld_wv"), sem("ld_wo")
        ld_w1, ld_w2, ld_vec = sem("ld_hid_w"), sem("ld_out_w"), sem("ld_vec")
        st_o = [sem(f"st_o{g}") for g in range(NG)]
        ld_o = [sem(f"ld_o{i}") for i in range(HALVES)]
        st_out = sem("st_out")
        whi_done, wlo_done, xhi_done, xlo_done = sem("whi_done"), sem("wlo_done"), sem("xhi_done"), sem("xlo_done")
        rows_done, w1hi_done, w1lo_done, w2hi_done, w2lo_done = (
            sem("rows_done"), sem("w1hi_done"), sem("w1lo_done"), sem("w2hi_done"), sem("w2lo_done"))
        pe_tok, pe_amat, pe_xT, pe_T, pe_v, pe_s, pe_pT, pe_oT, pe_o2T, pe_y = (
            sem(n) for n in ("pe_tok", "pe_amat", "pe_xT", "pe_T", "pe_v", "pe_s", "pe_pT", "pe_oT", "pe_o2T", "pe_y"))
        pe_x2T, pe_h2T, pe_p, pe_ev, pe_e4, pe_f1, pe_g, pe_f2 = (
            sem(n) for n in ("pe_x2T", "pe_h2T", "pe_p", "pe_ev", "pe_e4", "pe_f1", "pe_g", "pe_f2"))
        h_ready, var_ready, rstd_ready, xn_ready, amat_ready, xT_ready, tT_ready, v_ready = (
            sem(n) for n in ("h_ready", "var_ready", "rstd_ready", "xn_ready", "amat_ready", "xT_ready",
                             "tT_ready", "v_ready"))
        sc_ready, exp_ready, pr_ready, pT_ready, oT_ready, o2T_ready, h2_ready = (
            sem(n) for n in ("sc_ready", "exp_ready", "pr_ready", "pT_ready", "oT_ready", "o2T_ready", "h2_ready"))
        x2T_first, x2T_second, x2s_ready, h2T_ready, pscaled_ready, pm_ready, ev_ready, odd1_hi_ready, odd1_lo_ready, even1_ready, even2_ready, odd2_ready, e4_ready, gelu_ready, gs_ready, gm_ready, out_ready = (
            sem(n) for n in ("x2T_first", "x2T_second", "x2s_ready", "h2T_ready", "pscaled_ready", "pm_ready", "ev_ready",
                             "odd1_hi_ready", "odd1_lo_ready", "even1_ready", "even2_ready", "odd2_ready", "e4_ready",
                             "gelu_ready", "gs_ready", "gm_ready", "out_ready"))
        init_done, mv_init, dve_chain, warm_ready = sem("init_done"), sem("mv_init"), sem("dve_chain"), sem("warm_ready")

        def factors(half, first, c):
            return x2T[:, half, c, :].rearrange("p (b s) -> p s b", s=S)[:, first:first + 2 * RANK - 1:2, :]

        def inner(t):
            return t.unsqueeze(2).to_broadcast([P, RANK, 4, HB])

        def outer(t):
            return t.unsqueeze(1).to_broadcast([P, RANK, RANK, HB])

        def four(t):
            return t.rearrange("p (i r b) -> p i r b", i=RANK, b=HB)

        block = ctx.enter_context(nc.Block())

        @block.sync
        def _(sync):
            for i in range(PIECES):
                k = slice(PK * i, PK * (i + 1))
                sync.dma_start(w[:, k, :], w_t[:, k, :]).then_inc(ld_w[i], 16)
                sync.dma_start(xr[:, 0, k, :], x_t[0, :, k, :]).then_inc(ld_x[i], 16)
            sync.dma_start(con[:, :], consts).then_inc(ld_con, 16)
            sync.dma_start(add_rows[0:NROWS, :], rows).then_inc(ld_rows, 16)
            sync.dma_start(add_rows[LO_ROWS:LO_ROWS + NROWS, :], rows).then_inc(ld_rows, 16)
            sync.dma_start(wq_sb[:, :, :], wq).then_inc(ld_qk, 16)
            sync.dma_start(wk_sb[:, :, :], wk).then_inc(ld_qk, 16)
            for i in range(PIECES):
                k = slice(PK * i, PK * (i + 1))
                sync.dma_start(xr[:, 1, k, :], x_t[1, :, k, :]).then_inc(ld_x[PIECES + i], 16)
            sync.dma_start(wv_sb[:, :, :], wv_t).then_inc(ld_wv, 16)
            sync.dma_start(w1[:, :, :], w1_t).then_inc(ld_w1, 16)
            sync.dma_start(wo_sb[:, :, :], wo_t).then_inc(ld_wo, 16)
            sync.dma_start(w2[:, :, :], w2_t).then_inc(ld_w2, 16)
            sync.dma_start(b1_sb[:, :], b1_t).then_inc(ld_vec, 16)
            sync.dma_start(b2_sb[:, :], b2_t).then_inc(ld_vec, 16)
            sync.dma_start(scale_sb[:, :], scale.to_broadcast([P, 1])).then_inc(ld_vec, 16)
            for half in range(HALVES):
                groups = range(half * GH, (half + 1) * GH)
                for g in groups:
                    b0, nb = images_of(g)
                    b0 += HB * half
                    sync.wait_ge(oT_ready, g + 1)
                    for c in range(DC):
                        sync.dma_start(scratch[b0:b0 + nb, P * c:P * (c + 1), :].rearrange("b e q -> e b q"),
                                       oT[:, g, c, 0:nb * S].rearrange("p (b q) -> p b q", q=S)).then_inc(st_o[g], 16)
                for g in groups:
                    sync.wait_ge(st_o[g], 16 * DC)
                sync.dma_start(o2[half], scratch[HB * half:HB * (half + 1), :, :].rearrange("b e q -> (b e q)")
                               .rearrange("(o r d) -> r o d", o=OB, d=D)).then_inc(ld_o[half], 16)
            for half in range(HALVES):
                for c in range(DC):
                    sync.wait_ge(out_ready, half * DC + c + 1)
                    sync.dma_start(out_t[c, :, half * HT:(half + 1) * HT], outT[:, half, c, :]).then_inc(st_out, 16)
            sync.wait_ge(st_out, 16 * HALVES * DC)

        @block.gpsimd
        def _(pool):
            nc.gpsimd.memset(expo[:, :], -0.5).then_inc(init_done, 1)
            nc.gpsimd.memset(warm_in[:, :], 0.0).then_inc(warm_ready, 1)
            nc.gpsimd.memset(mv[:, :, :, :], 1.0).then_inc(mv_init, 1)
            pool.wait_ge(init_done, 1)

            def powers(n):
                pool.wait_ge(var_ready, n + 1)
                nc.gpsimd.tensor_tensor(rstd[:, n, :], ve[:, n, :], expo[:, :], ALU.pow).then_inc(rstd_ready, 1)

            for n in range(3):
                powers(n)

            def second_factors(half):
                pool.wait_ge(x2T_first, half + 1)
                pool.wait_ge(x2T_second, half + 1)
                for c in range(DC):
                    nc.gpsimd.tensor_copy(four(even2[:, half, c, :]), outer(factors(half, 9, c))).then_inc(even2_ready, 1)
                for c in range(DC):
                    nc.gpsimd.tensor_copy(odd2[:, half, c, :].rearrange("p (i b) -> p i b", i=RANK),
                                          factors(half, 10, c)).then_inc(odd2_ready, 1)

            second_factors(0)
            powers(3)
            second_factors(1)

        @block.scalar
        def _(act):
            act.wait_ge(init_done, 1)
            nc.scalar.activation(warm[0:1, 0:1], expo[0:1, 0:1], ACT.Exp)

            def x_high(i):
                act.wait_ge(ld_x[i], 16)
                half, k = i // PIECES, slice(PK * (i % PIECES), PK * (i % PIECES + 1))
                nc.scalar.copy(x_hi[:, half, k, :], xr[:, half, k, :]).then_inc(xhi_done, 1)

            def w_high(i):
                act.wait_ge(ld_w[i], 16)
                k = slice(PK * i, PK * (i + 1))
                nc.scalar.copy(w_hi[:, k, :], w[:, k, :]).then_inc(whi_done, 1)

            def h_rows(g):
                n = span(g)[1]
                act.wait_ge(pe_tok, g + 1)
                nc.scalar.copy(h[0:n, g, :], tok_bank(g)[0:n, 0:D]).then_inc(h_ready, 1)

            def move_xT(half):
                act.wait_ge(pe_xT, DC * half + 1)
                nc.scalar.copy(xT[:, half, 0, :], xT_bank(half, 0)[:, 0:HT]).then_inc(xT_ready, 1)

            def move_v(g):
                n = span(g)[1]
                act.wait_ge(pe_v, g + 1)
                nc.scalar.copy(v[0:n, g, :], v_bank(g)[0:n, 0:D]).then_inc(v_ready, 1)

            def exps(g):
                n = span(g)[1]
                act.wait_ge(sc_ready, g + 1)
                nc.scalar.activation(pr[0:n, g, 0:n], sc[0:n, g, 0:n], ACT.Exp, bias=negmax[0:n, g:g + 1],
                                     scale=-1.0, accum_out=rsum[0:n, g:g + 1]).then_inc(exp_ready, 1)

            def move_oT(g):
                n = span(g)[1]
                act.wait_ge(pe_oT, g + 1)
                nc.scalar.copy(oT[:, g, :, 0:n], oT_bank(g)[:, 0:DC * n].rearrange("p (c t) -> p c t", c=DC))\
                    .then_inc(oT_ready, 1)

            def move_o2T(half, c):
                act.wait_ge(pe_o2T, DC * half + c + 1)
                nc.scalar.copy(o2T[:, half, c, :], o2T_bank(half, c)[:, 0:HT]).then_inc(o2T_ready, 1)

            def move_x2T(half):
                act.wait_ge(pe_x2T, DC * half + 1)
                nc.scalar.copy(x2T[:, half, 0, :], end_bank[0][:, 0:HT]).then_inc(x2T_first, 1)

            def first_factors(half):
                act.wait_ge(x2T_first, half + 1)
                act.wait_ge(x2T_second, half + 1)
                if half:
                    act.wait_ge(pe_p, half)
                    act.wait_ge(pe_ev, half)
                for c in range(DC):
                    nc.scalar.copy(four(odd1_hi[:, c, :]), inner(factors(half, 2, c))).then_inc(odd1_hi_ready, 1)
                for c in range(DC):
                    nc.scalar.copy(four(even1[:, c, :]), inner(factors(half, 1, c))).then_inc(even1_ready, 1)

            def move_h2T(half):
                for c in range(DC):
                    act.wait_ge(pe_h2T, DC * half + c + 1)
                    nc.scalar.copy(h2T[:, half, c, :], end_bank[c][:, 0:HT]).then_inc(h2T_ready, 1)

            def scaled(half):
                act.wait_ge(pe_p, half + 1)
                if half:
                    act.wait_ge(pm_ready, half)
                nc.scalar.mul(pscaled[:, :], odd_bank[:, 0:HT], scale_sb[:, 0:1]).then_inc(pscaled_ready, 1)

            def gelus(half, ks):
                for k in ks:
                    act.wait_ge(pe_f1, HC * half + k + 1)
                    if half:
                        act.wait_ge(pe_g, 1)
                    nc.scalar.activation(gr[:, k, :], hid_bank(k)[:, 0:HT], ACT.Gelu,
                                         bias=b1_sb[:, k:k + 1]).then_inc(gelu_ready, 1)

            def w1_high(c):
                act.wait_ge(ld_w1, 16)
                nc.scalar.copy(w1_hi[:, c, :], w1[:, c, :]).then_inc(w1hi_done, 1)

            def w2_high(c):
                act.wait_ge(ld_w2, 16)
                k = slice(4 * c, 4 * c + 4)
                nc.scalar.copy(w2_hi[:, k, :], w2[:, k, :]).then_inc(w2hi_done, 1)

            for i in range(1, PIECES):
                w_high(i)
                x_high(i)
            w_high(0)
            for i in range(PIECES, 2 * PIECES):
                x_high(i)
            for g in range(GH + 1):
                h_rows(g)
            move_xT(0)
            h_rows(4)
            h_rows(5)
            for g in range(GH):
                move_v(g)
            move_xT(1)
            for g in range(GH):
                exps(g)
            w1_high(0)
            move_v(3)
            for g in range(GH):
                move_oT(g)
            for g in range(GH, NG):
                exps(g)
            move_v(4)
            move_v(5)
            w1_high(1)
            for g in range(GH, NG):
                move_oT(g)
            w2_high(0)
            move_o2T(0, 0)
            w2_high(1)
            nc.scalar.activation(warm[0:1, 1:2], expo[0:1, 0:1], ACT.Gelu)
            move_o2T(1, 0)
            move_o2T(1, 1)
            act.wait_ge(ld_vec, 48)
            move_x2T(0)
            first_factors(0)
            scaled(0)
            gelus(0, range(4))
            move_x2T(1)
            gelus(0, range(4, 6))
            first_factors(1)
            move_h2T(0)
            gelus(0, range(6, HC))
            move_h2T(1)
            scaled(1)
            gelus(1, range(HC))

        @block.vector
        def _(dve):
            chained = [0]

            def then(instruction):
                chained[0] += 1
                instruction.then_inc(dve_chain, 1)
                dve.wait_ge(dve_chain, chained[0])

            def w_low(i):
                k = slice(PK * i, PK * (i + 1))
                dve.wait_ge(ld_w[i], 16)
                dve.wait_ge(whi_done, i if i else PIECES)
                nc.vector.tensor_tensor(w_lo[:, k, :], w[:, k, :], w_hi[:, k, :], ALU.subtract).then_inc(wlo_done, 1)

            def x_low(i):
                half, k = i // PIECES, slice(PK * (i % PIECES), PK * (i % PIECES + 1))
                dve.wait_ge(ld_x[i], 16)
                dve.wait_ge(xhi_done, i)
                nc.vector.tensor_tensor(x_lo[:, half, k, :], xr[:, half, k, :], x_hi[:, half, k, :],
                                        ALU.subtract).then_inc(xlo_done, 1)

            def norm_stats(n, rows_, ready, g):
                t, i = span(g)[1], g % GH
                dve.wait_ge(ready, g + 1)
                then(nc.vector.bn_stats(stats[0:t, n, i, :], rows_[0:t, g, :]))
                nc.vector.bn_aggr(mv[0:t, n, i, :], stats[0:t, n, i, :]).then_inc(dve_chain, 1)
                chained[0] += 1

            def norm_var(n):
                dve.wait_ge(dve_chain, chained[0])
                nc.vector.tensor_scalar(ve[:, n, :], mv[:, n, :, 1], EPS, None, ALU.add).then_inc(var_ready, 1)

            def norm_rows(n, rows_, g):
                t, i = span(g)[1], g % GH
                dve.wait_ge(rstd_ready, n + 1)
                if n >= HALVES:
                    dve.wait_ge(pe_xT, DC * (n - 1))
                nc.vector.tensor_scalar(xn[0:t, g, :], rows_[0:t, g, :], mv[0:t, n, i, 0:1], rstd[0:t, n, i:i + 1],
                                        ALU.subtract, ALU.mult).then_inc(xn_ready, 1)

            def move_xT(half):
                dve.wait_ge(pe_xT, DC * half + DC)
                nc.vector.tensor_copy(xT[:, half, 1, :], xT_bank(half, 1)[:, 0:HT]).then_inc(xT_ready, 1)

            def move_o2T(half, c):
                dve.wait_ge(pe_o2T, DC * half + c + 1)
                nc.vector.tensor_copy(o2T[:, half, c, :], o2T_bank(half, c)[:, 0:HT]).then_inc(o2T_ready, 1)

            def move_T(half):
                for c in range(DC):
                    dve.wait_ge(pe_T, DC * half + c + 1)
                    nc.vector.tensor_copy(tT[:, half, c, :], t_bank(half, c)[:, 0:HT]).then_inc(tT_ready, 1)

            def masked_max(g):
                nb = images_of(g)[1]
                n = nb * S
                dve.wait_ge(pe_s, g + 1)
                nc.vector.tensor_tensor_reduce(
                    out=sc[0:n, g, 0:n].rearrange("p (b k) -> p b k", k=S),
                    in0=score_bank(g)[0:n, 0:n].rearrange("p (b k) -> p b k", k=S),
                    in1=con[0:n, C_ATT:C_ATT + nb].unsqueeze(2).to_broadcast([n, nb, S]),
                    scale=1.0, scalar=3e38, op0=ALU.add, op1=ALU.min,
                    accum_out=negmax[0:n, g:g + 1]).then_inc(sc_ready, 1)

            def softmax_end(g):
                n = span(g)[1]
                dve.wait_ge(exp_ready, g + 1)
                then(nc.vector.reciprocal(rinv[0:n, g:g + 1], rsum[0:n, g:g + 1]))
                nc.vector.tensor_scalar(pr[0:n, g, 0:n], pr[0:n, g, 0:n], rinv[0:n, g:g + 1], None,
                                        ALU.mult).then_inc(pr_ready, 1)

            def move_pT(g):
                n = span(g)[1]
                dve.wait_ge(pe_pT, g + 1)
                nc.vector.tensor_copy(pT[0:n, g, 0:n], pT_bank(g)[0:n, 0:n]).then_inc(pT_ready, 1)

            def residual(g):
                n = span(g)[1]
                dve.wait_ge(pe_y, g + 1)
                nc.vector.tensor_tensor(h2[0:n, g, :], y_bank(g)[0:n, 0:D], h[0:n, g, :], ALU.add)\
                    .then_inc(h2_ready, 1)

            def second_T(half):
                dve.wait_ge(pe_x2T, DC * half + DC)
                nc.vector.tensor_copy(x2T[:, half, 1, :], end_bank[1][:, 0:HT]).then_inc(x2T_second, 1)

            def split_x2(half):
                for c in range(DC):
                    dve.wait_ge((x2T_first, x2T_second)[c], half + 1)
                    then(nc.vector.tensor_copy(x2_hi[:, half, c, :], x2T[:, half, c, :]))
                    nc.vector.tensor_tensor(x2_lo[:, half, c, :], x2T[:, half, c, :], x2_hi[:, half, c, :],
                                            ALU.subtract).then_inc(x2s_ready, 1)

            def odd_low(half):
                for c in range(DC):
                    dve.wait_ge(odd1_hi_ready, DC * half + c + 1)
                    nc.vector.tensor_tensor(four(odd1_lo[:, c, :]), inner(factors(half, 2, c)),
                                            four(odd1_hi[:, c, :]), ALU.subtract).then_inc(odd1_lo_ready, 1)

            def factors_ready(half):
                dve.wait_ge(pe_ev, half + 1)
                then(nc.vector.tensor_copy(ev_raw[:, :], even_bank[:, 0:D]))
                then(nc.vector.tensor_copy(ev_hi[:, :], ev_raw[:, :]))
                nc.vector.scalar_tensor_tensor(out=ev[:, half, :], in0=ev_raw[:, :],
                                               scalar=con[:, C_SE:C_SE + 1], in1=ev_hi[:, :],
                                               op0=ALU.mult, op1=ALU.subtract).then_inc(ev_ready, 1)

            def second_even(half):
                dve.wait_ge(pe_e4, half + 1)
                for j in range(RANK):
                    rows_ = slice(32 * j, 32 * (j + 1))
                    last = nc.vector.tensor_tensor(
                        e4[rows_, half, :].rearrange("p (i o) -> p i o", i=RANK),
                        even_bank[rows_, j:D:RANK].unsqueeze(1).to_broadcast([32, RANK, D // RANK]),
                        con[rows_, C_IM:C_IM + RANK].unsqueeze(2).to_broadcast([32, RANK, D // RANK]), ALU.mult)
                last.then_inc(e4_ready, 1)

            def projection_parts(half):
                dve.wait_ge(pscaled_ready, half + 1)
                then(nc.vector.tensor_copy(p_hi[:, :], pscaled[:, :]))
                then(nc.vector.scalar_tensor_tensor(out=p_part[:, :], in0=pscaled[:, :],
                                                    scalar=con[:, C_SP:C_SP + 1], in1=p_hi[:, :],
                                                    op0=ALU.mult, op1=ALU.subtract))
                nc.vector.tensor_tensor(
                    pm[:, half, :].rearrange("p (b s) -> p b s", s=S),
                    p_part[:, :].rearrange("p (b s) -> p b s", s=S),
                    con[:, C_PM:C_PM + HB].unsqueeze(2).to_broadcast([P, HB, S]), ALU.mult).then_inc(pm_ready, 1)

            def split_g(half, ks):
                for k in ks:
                    dve.wait_ge(gelu_ready, HC * half + k + 1)
                    if half:
                        dve.wait_ge(pe_f2, DC)
                    then(nc.vector.tensor_copy(g_hi[:, k, :], gr[:, k, :]))
                    nc.vector.tensor_tensor(g_lo[:, k, :], gr[:, k, :], g_hi[:, k, :], ALU.subtract)\
                        .then_inc(gs_ready, 1)

            def mask_g(half):
                dve.wait_ge(pe_g, half + 1)
                nc.vector.scalar_tensor_tensor(
                    out=gm[:, half, :].rearrange("p (b s) -> p b s", s=S),
                    in0=odd_bank[:, 0:HT].rearrange("p (b s) -> p b s", s=S), scalar=scale_sb[:, 0:1],
                    in1=con[:, C_GM:C_GM + HB].unsqueeze(2).to_broadcast([P, HB, S]),
                    op0=ALU.mult, op1=ALU.mult).then_inc(gm_ready, 1)

            def finish(half):
                for c in range(DC):
                    dve.wait_ge(pe_f2, DC * half + c + 1)
                    dve.wait_ge(h2T_ready, DC * half + c + 1)
                    nc.vector.scalar_tensor_tensor(out=outT[:, half, c, :], in0=end_bank[c][:, 0:HT],
                                                   scalar=b2_sb[:, c:c + 1], in1=h2T[:, half, c, :],
                                                   op0=ALU.add, op1=ALU.add).then_inc(out_ready, 1)

            def w1_low(c):
                dve.wait_ge(w1hi_done, c + 1)
                nc.vector.tensor_tensor(w1_lo[:, c, :], w1[:, c, :], w1_hi[:, c, :], ALU.subtract).then_inc(w1lo_done, 1)

            def w2_low(c):
                k = slice(4 * c, 4 * c + 4)
                dve.wait_ge(w2hi_done, c + 1)
                nc.vector.tensor_tensor(w2_lo[:, k, :], w2[:, k, :], w2_hi[:, k, :], ALU.subtract).then_inc(w2lo_done, 1)

            then(nc.vector.memset(add_hl[:, :].bitcast(F32), 0.0))
            for i in range(1, PIECES):
                w_low(i)
                x_low(i)
            dve.wait_ge(ld_con, 16)
            nc.vector.tensor_copy(ind[:, :], con[0:LO_ROWS + NROWS, C_IND:C_IND + GT])
            dve.wait_ge(ld_rows, 32)
            then(nc.vector.tensor_copy(add_hl[LO_ROWS:LO_ROWS + NROWS, :], add_rows[LO_ROWS:LO_ROWS + NROWS, :]))
            nc.vector.tensor_copy(add_hl[0:NROWS, :], add_rows[0:NROWS, :])
            nc.vector.tensor_tensor(add_hl[LO_ROWS:LO_ROWS + NROWS, :], add_rows[LO_ROWS:LO_ROWS + NROWS, :],
                                    add_hl[LO_ROWS:LO_ROWS + NROWS, :], ALU.subtract).then_inc(rows_done, 1)
            w_low(0)
            for i in range(PIECES, 2 * PIECES):
                x_low(i)
            dve.wait_ge(mv_init, 1)
            for g in range(GH):
                norm_stats(0, h, h_ready, g)
            norm_var(0)
            dve.wait_ge(pe_amat, 1)
            nc.vector.tensor_scalar(amat[:, :, :].rearrange("p c d -> p (c d)"), bank[5][:, :], -0.25, None,
                                    ALU.mult).then_inc(amat_ready, 1)
            for g in range(GH):
                norm_rows(0, h, g)
            move_xT(0)
            for g in range(GH, NG):
                norm_stats(1, h, h_ready, g)
            norm_var(1)
            move_T(0)
            for g in range(GH, NG):
                norm_rows(1, h, g)
            for g in range(GH):
                masked_max(g)
            move_xT(1)
            for g in range(GH):
                softmax_end(g)
            move_T(1)
            for g in range(GH):
                move_pT(g)
            w1_low(0)
            for g in range(GH, NG):
                masked_max(g)
            for g in range(GH, NG):
                softmax_end(g)
            for g in range(GH, NG):
                move_pT(g)
            w1_low(1)
            w2_low(0)
            move_o2T(0, 1)
            w2_low(1)
            for g in range(GH):
                residual(g)
                norm_stats(2, h2, h2_ready, g)
            norm_var(2)
            for g in range(GH):
                norm_rows(2, h2, g)
            residual(3)
            residual(4)
            second_T(0)
            residual(5)
            split_x2(0)
            odd_low(0)
            dve.wait_ge(ld_vec, 48)
            for g in range(GH, NG):
                norm_stats(3, h2, h2_ready, g)
            norm_var(3)
            factors_ready(0)
            projection_parts(0)
            for g in range(GH, NG):
                norm_rows(3, h2, g)
            split_g(0, range(4))
            second_T(1)
            split_g(0, range(4, 6))
            split_x2(1)
            odd_low(1)
            split_g(0, range(6, HC))
            factors_ready(1)
            projection_parts(1)
            second_even(0)
            mask_g(0)
            finish(0)
            split_g(1, range(HC))
            second_even(1)
            mask_g(1)
            finish(1)

        @block.tensor
        def _(pe):
            ident = con[:, C_ID:C_ID + P]

            def three(out, s_hi, s_lo, m_hi, m_lo, start, stop):
                nc.tensor.matmul(out, s_lo, m_hi, start=start, stop=False)
                nc.tensor.matmul(out, s_hi, m_lo, start=False, stop=False)
                return nc.tensor.matmul(out, s_hi, m_hi, start=False, stop=stop)

            def tok_piece(g, i):
                half, (cols, n) = g // GH, span(g)
                for k in range(PK * i, PK * (i + 1)):
                    three(tok_bank(g)[0:n, 0:D], x_hi[:, half, k, cols], x_lo[:, half, k, cols],
                          w_hi[:, k, :], w_lo[:, k, :], k == 0, False)

            def tok_rows(g):
                n = span(g)[1]
                pe.wait_ge(rows_done, 1)
                nc.tensor.matmul(tok_bank(g)[0:n, 0:D], ind[:, 0:n], add_hl[:, :], start=False, stop=True)\
                    .then_inc(pe_tok, 1)

            def tok_group(g):
                pe.wait_ge(h_ready, g - GH + 1)
                pe.wait_ge(whi_done, PIECES)
                pe.wait_ge(wlo_done, PIECES)
                pe.wait_ge(xhi_done, 2 * PIECES - 1)
                pe.wait_ge(xlo_done, 2 * PIECES - 1)
                for i in range(PIECES):
                    tok_piece(g, i)
                tok_rows(g)

            def to_T(rows_, half, c, out, done, ready=None, before=0):
                for g in range(half * GH, (half + 1) * GH):
                    cols, n = span(g)
                    if ready is not None:
                        pe.wait_ge(ready, before + g + 1)
                    last = nc.tensor.transpose(out[:, cols], rows_[0:n, g, P * c:P * (c + 1)], ident[0:n, 0:n])
                last.then_inc(done, 1)

            def x_T(half):
                if half:
                    pe.wait_ge(h_ready, NG)
                    pe.wait_ge(tT_ready, DC)
                for c in range(DC):
                    to_T(xn, half, c, xT_bank(half, c), pe_xT, xn_ready)

            def t_T(half):
                pe.wait_ge(amat_ready, 1)
                pe.wait_ge(xT_ready, DC * (half + 1))
                if half:
                    pe.wait_ge(v_ready, 2)
                for c in range(DC):
                    for k in range(DC):
                        last = nc.tensor.matmul(t_bank(half, c)[:, 0:HT], amat[:, k, P * c:P * (c + 1)],
                                                xT[:, half, k, :], start=k == 0, stop=k == DC - 1)
                    last.then_inc(pe_T, 1)

            def values(g):
                half, (cols, n) = g // GH, span(g)
                pe.wait_ge(ld_wv, 16)
                pe.wait_ge(*((h_ready, GH), (h_ready, 4), (h_ready, 5), (sc_ready, GH), (pT_ready, GH), (v_ready, 4))[g])
                for k in range(DC):
                    last = nc.tensor.matmul(v_bank(g)[0:n, 0:D], xT[:, half, k, cols], wv_sb[:, k, :],
                                            start=k == 0, stop=k == DC - 1)
                last.then_inc(pe_v, 1)

            def scores(g):
                half, (cols, n) = g // GH, span(g)
                pe.wait_ge(tT_ready, DC * (half + 1))
                if half:
                    pe.wait_ge(pT_ready, max(1, g - GH))
                for k in range(DC):
                    last = nc.tensor.matmul(score_bank(g)[0:n, 0:n], tT[:, half, k, cols], xT[:, half, k, cols],
                                            start=k == 0, stop=k == DC - 1)
                last.then_inc(pe_s, 1)

            def attend_T(g):
                n = span(g)[1]
                pe.wait_ge(pr_ready, g + 1)
                pe.wait_ge(*((v_ready, 3), (sc_ready, 1), (sc_ready, 2), (oT_ready, 1), (oT_ready, 2), (oT_ready, 3))[g])
                nc.tensor.transpose(pT_bank(g)[0:n, 0:n], pr[0:n, g, 0:n], ident[0:n, 0:n]).then_inc(pe_pT, 1)

            def attend(g):
                n = span(g)[1]
                pe.wait_ge(pT_ready, g + 1)
                pe.wait_ge(v_ready, g + 1)
                pe.wait_ge(*((xT_ready, 4), (xT_ready, 4), (tT_ready, 3), (sc_ready, 4), (sc_ready, 5), (sc_ready, 6))[g])
                for c in range(DC):
                    last = nc.tensor.matmul(oT_bank(g)[:, c * n:(c + 1) * n], v[0:n, g, P * c:P * (c + 1)],
                                            pT[0:n, g, 0:n], start=True, stop=True)
                last.then_inc(pe_oT, 1)

            def o2_T(half):
                pe.wait_ge(*((v_ready, NG), (oT_ready, 5))[half])
                pe.wait_ge(ld_o[half], 16)
                for c in range(DC):
                    for i in range(OB):
                        last = nc.tensor.transpose(o2T_bank(half, c)[:, OR * i:OR * (i + 1)],
                                                   o2[half][:, i, P * c:P * (c + 1)], ident[0:OR, 0:OR])
                    last.then_inc(pe_o2T, 1)

            def project(g):
                half, (cols, n) = g // GH, span(g)
                pe.wait_ge(ld_wo, 16)
                pe.wait_ge(o2T_ready, DC * (half + 1))
                pe.wait_ge(*((pT_ready, 4), (pT_ready, 5), (pT_ready, 6), (oT_ready, NG), (o2T_ready, DC),
                             (o2T_ready, DC))[g])
                for k in range(DC):
                    last = nc.tensor.matmul(y_bank(g)[0:n, 0:D], o2T[:, half, k, cols], wo_sb[:, k, :],
                                            start=k == 0, stop=k == DC - 1)
                last.then_inc(pe_y, 1)

            def x2_T(half):
                if half == 0:
                    pe.wait_ge(h2_ready, 2)
                else:
                    pe.wait_ge(x2T_first, 1)
                    pe.wait_ge(x2T_second, 1)
                for c in range(DC):
                    to_T(xn, half, c, end_bank[c], pe_x2T, xn_ready, NG)

            def h2_T(half):
                if half == 0:
                    pe.wait_ge(x2T_first, 2)
                    pe.wait_ge(x2T_second, 2)
                else:
                    pe.wait_ge(h2T_ready, DC)
                for c in range(DC):
                    to_T(h2, half, c, end_bank[c], pe_h2T)

            def low_rank(half):
                pe.wait_ge(even1_ready, DC * (half + 1))
                if half:
                    pe.wait_ge(ev_ready, 1)
                else:
                    pe.wait_ge(o2T_ready, DC * HALVES)
                for c in range(DC):
                    last = nc.tensor.transpose(even_bank[:, P * c:P * (c + 1)], even1[:, c, :], ident)
                last.then_inc(pe_ev, 1)
                pe.wait_ge(x2s_ready, DC * (half + 1))
                pe.wait_ge(odd1_lo_ready, DC * (half + 1))
                pe.wait_ge(*((h2_ready, GH), (pscaled_ready, 1))[half])
                for c in range(DC):
                    last = three(odd_bank[:, 0:HT], odd1_hi[:, c, :], odd1_lo[:, c, :], x2_hi[:, half, c, :],
                                 x2_lo[:, half, c, :], c == 0, c == DC - 1)
                last.then_inc(pe_p, 1)

            def second_even_rows(half):
                pe.wait_ge(even2_ready, DC * (half + 1))
                pe.wait_ge(ev_ready, HALVES)
                for c in range(DC):
                    last = nc.tensor.transpose(even_bank[:, P * c:P * (c + 1)], even2[:, half, c, :], ident)
                last.then_inc(pe_e4, 1)

            def hidden(half, k):
                pe.wait_ge(w1lo_done, DC)
                pe.wait_ge(x2s_ready, DC * (half + 1))
                if k >= 4:
                    pe.wait_ge(gelu_ready, HC * half + k - 3)
                elif half:
                    pe.wait_ge(gelu_ready, HC - 3 + k)
                else:
                    pe.wait_ge(*((o2T_ready, DC * HALVES), (h2_ready, 4), (h2_ready, 5), (h2_ready, 6))[k])
                cols = slice(P * k, P * (k + 1))
                for c in range(DC):
                    three(hid_bank(k)[:, 0:HT], w1_hi[:, c, cols], w1_lo[:, c, cols], x2_hi[:, half, c, :],
                          x2_lo[:, half, c, :], c == 0, False)

            def hidden_low_rank(half, k):
                i, c = k // 2, k % 2
                pe.wait_ge(pm_ready, half + 1)
                pe.wait_ge(ev_ready, half + 1)
                nc.tensor.matmul(hid_bank(k)[:, 0:HT], ev[32 * i:32 * (i + 1), half, P * c:P * (c + 1)],
                                 pm[32 * i:32 * (i + 1), half, :], start=False, stop=True).then_inc(pe_f1, 1)

            def output(half, ks):
                if half == 0:
                    pe.wait_ge(h2T_ready, DC * HALVES)
                else:
                    pe.wait_ge(out_ready, DC)
                for k in ks:
                    pe.wait_ge(w2lo_done, k // 4 + 1)
                    pe.wait_ge(gs_ready, HC * half + k + 1)
                    for c in range(DC):
                        cols = slice(P * c, P * (c + 1))
                        three(end_bank[c][:, 0:HT], w2_hi[:, k, cols], w2_lo[:, k, cols], g_hi[:, k, :], g_lo[:, k, :],
                              k == 0, False)

            def hidden_on_odd(half):
                pe.wait_ge(gelu_ready, HC * (half + 1))
                pe.wait_ge(odd2_ready, DC * (half + 1))
                pe.wait_ge(pscaled_ready, HALVES)
                for c in range(DC):
                    for j in range(RANK):
                        last = nc.tensor.matmul(odd_bank[32 * j:32 * (j + 1), 0:HT], odd2[:, half, c, :],
                                                gr[:, DC * j + c, :], start=c == 0, stop=c == DC - 1)
                last.then_inc(pe_g, 1)

            def output_low_rank(half):
                pe.wait_ge(gm_ready, half + 1)
                pe.wait_ge(e4_ready, half + 1)
                for c in range(DC):
                    nc.tensor.matmul(end_bank[c][:, 0:HT], e4[:, half, P * c:P * (c + 1)], gm[:, half, :],
                                     start=False, stop=True).then_inc(pe_f2, 1)

            pe.wait_ge(warm_ready, 1)
            for _ in range(WARM):
                nc.tensor.matmul(bank[7][:, 0:P], warm_in[:, :], warm_in[:, :], start=True, stop=True)
            pe.wait_ge(ld_w[0], 16)
            pe.wait_ge(ld_x[0], 16)
            for g in range(GH):
                cols, n = span(g)
                for k in range(PK):
                    nc.tensor.matmul(tok_bank(g)[0:n, 0:D], xr[:, 0, k, cols], w[:, k, :], start=k == 0, stop=False)
            for i in range(1, PIECES):
                pe.wait_ge(wlo_done, i)
                pe.wait_ge(xlo_done, i)
                for g in range(GH):
                    tok_piece(g, i)
            for g in range(GH):
                tok_rows(g)
            pe.wait_ge(ld_qk, 32)
            pe.wait_ge(ld_con, 16)
            for c in range(DC):
                for k in range(DC):
                    last = nc.tensor.matmul(bank[5][:, D * c:D * (c + 1)], wq_sb[:, k, P * c:P * (c + 1)],
                                            wk_sb[:, k, :], start=k == 0, stop=k == DC - 1)
            last.then_inc(pe_amat, 1)
            tok_group(3)
            x_T(0)
            tok_group(4)
            tok_group(5)
            t_T(0)
            for g in range(GH):
                values(g)
            for g in range(GH):
                scores(g)
            x_T(1)
            t_T(1)
            for g in range(GH):
                attend_T(g)
            values(3)
            for g in range(GH):
                attend(g)
            for g in range(GH, NG):
                scores(g)
            values(4)
            values(5)
            for g in range(GH, NG):
                attend_T(g)
            for g in range(GH, NG):
                attend(g)
            o2_T(0)
            for g in range(GH):
                project(g)
            o2_T(1)
            for g in range(GH, NG):
                project(g)
            x2_T(0)
            hidden(0, 0)
            hidden(0, 1)
            low_rank(0)
            hidden(0, 2)
            hidden(0, 3)
            for k in range(4):
                hidden_low_rank(0, k)
            x2_T(1)
            for k in range(4, 6):
                hidden(0, k)
                hidden_low_rank(0, k)
            h2_T(0)
            for k in range(6, HC):
                hidden(0, k)
                hidden_low_rank(0, k)
            h2_T(1)
            low_rank(1)
            output(0, range(HC))
            second_even_rows(0)
            hidden_on_odd(0)
            output_low_rank(0)
            for k in range(HC):
                hidden(1, k)
                hidden_low_rank(1, k)
            output(1, range(6))
            second_even_rows(1)
            hidden_on_odd(1)
            output(1, range(6, HC))
            output_low_rank(1)


def kernel(x, cls_tok, L0_tok_W, L0_tok_b, L0_tok_cls_token, L0_tok_pos_embedding, L0_attn_wq, L0_attn_wk,
           L0_attn_wv, L0_attn_wo, L0_ffn_W1, L0_ffn_b1, L0_ffn_W2, L0_ffn_b2, L0_ffn_scale):
    import concourse.bacc as bacc
    from concourse.bass_utils import run_bass_kernel_spmd

    def chunks(a):
        a = np.asarray(a)
        return np.ascontiguousarray(a.reshape(-1, P, a.shape[1]).transpose(1, 0, 2))

    n = IMG // PATCH
    patches = np.asarray(x).reshape(B, CH, n, PATCH, n, PATCH).transpose(0, 2, 4, 1, 3, 5).reshape(B, NPATCH, KD)
    tokens = np.zeros((B, S, KD), np.float32)
    tokens[:, S - NPATCH:, :] = patches
    x_t = tokens.reshape(HALVES, HT, KC, P).transpose(0, 3, 2, 1)
    rows = np.concatenate([np.asarray(cls_tok).reshape(1, D), np.asarray(L0_tok_cls_token).reshape(1, D),
                           np.asarray(L0_tok_b).reshape(1, D), np.asarray(L0_tok_pos_embedding).reshape(-1, D)])
    arrays = {
        "x_t": x_t, "w_t": chunks(np.asarray(L0_tok_W).T), "rows": rows, "consts": constants(),
        "wq": chunks(L0_attn_wq), "wk": chunks(L0_attn_wk),
        "wv_t": chunks(np.asarray(L0_attn_wv).T), "wo_t": chunks(np.asarray(L0_attn_wo).T),
        "w1_t": chunks(np.asarray(L0_ffn_W1).T), "w2_t": chunks(np.asarray(L0_ffn_W2).T),
        "b1_t": np.asarray(L0_ffn_b1).reshape(HC, P).T, "b2_t": np.asarray(L0_ffn_b2).reshape(DC, P).T,
        "scale": np.asarray(L0_ffn_scale).reshape(1, 1),
    }
    arrays = {k: np.ascontiguousarray(a) for k, a in arrays.items()}
    nc = bacc.Bacc("TRN2", target_bir_lowering=False, num_devices=1)
    args = [nc.dram_tensor(k, a.shape, mybir.dt.from_np(a.dtype), kind="ExternalInput").ap() for k, a in arrays.items()]
    out_t = nc.dram_tensor("out_t", (DC, P, B * S), F32, kind="ExternalOutput").ap()
    build(nc, *args, out_t)
    result = run_bass_kernel_spmd(nc, [arrays], core_ids=[0]).results[0]["out_t"]
    return np.ascontiguousarray(result.reshape(D, B, S).transpose(1, 2, 0))
```

```python
from contextlib import ExitStack

import numpy as np

import concourse.bass as bass
from concourse import mybir

F32 = mybir.dt.float32
F32R = mybir.dt.float32r
ALU = mybir.AluOpType
ACT = mybir.ActivationFunctionType

P = 128
B, CH, IMG, PATCH = 16, 3, 96, 16
NPATCH = (IMG // PATCH) ** 2
S = NPATCH + 2
D = 256
KD = CH * PATCH * PATCH
HID = 1024
EPS = 1e-5
KC, DC, HC = KD // P, D // P, HID // P
HALVES = 2
HB = B // HALVES
HT = HB * S
GROUP_IMAGES = (3, 3, 2)
GH = len(GROUP_IMAGES)
NG = HALVES * GH
GT = max(GROUP_IMAGES) * S
BLOCKS = (P, P, HT - 2 * P)
RANK = 4
PIECES = 3
PK = KC // PIECES
NROWS = 3 + 1 + NPATCH
LO_ROWS = 64
BANK = 512
WARM = 6
KEEP = 4
OFF_BLOCK = 1e30

C_ID = 0
C_ATT = C_ID + P
C_PM = C_ATT + 3
C_GM = C_PM + HB
C_IM = C_GM + HB
C_SE = C_IM + RANK
C_SP = C_SE + 1
C_IND = C_SP + 1
NCONST = C_IND + GT


def constants():
    c = np.zeros((P, NCONST), np.float32)
    c[:, C_ID:C_ID + P] = np.eye(P)
    tok = np.arange(GT) // S
    c[:GT, C_ATT:C_ATT + 3] = np.where(tok[:, None] == np.arange(3)[None], 0.0, OFF_BLOCK)
    p = np.arange(P)
    b, r = p % HB, (p // HB) % 4
    own = (b[:, None] == np.arange(HB)[None]).astype(np.float32)
    c[:, C_PM:C_PM + HB] = own * np.array([1.0, -1.0, -1.0, 1.0])[r][:, None]
    c[:, C_GM:C_GM + HB] = own
    c[:, C_IM:C_IM + RANK] = ((p // HB) % RANK)[:, None] == np.arange(RANK)[None]
    c[:, C_SE] = r >= 2
    c[:, C_SP] = r % 2
    for t in range(GT):
        s = t % S
        for row in ([0] if s == 0 else [1, 3] if s == 1 else [2, 2 + s]):
            c[row, C_IND + t] = 1.0
            c[LO_ROWS + row, C_IND + t] = 1.0
    return c


def images_of(g):
    return sum(GROUP_IMAGES[:g % GH]), GROUP_IMAGES[g % GH]


def span(g):
    b0, nb = images_of(g)
    return slice(b0 * S, (b0 + nb) * S), nb * S


def build(nc, x_t, w_t, rows, consts, wq, wk, wv_t, wo_t, w1_t, w2_t, b1_t, b2_t, scale, out_t):
    ctx = ExitStack()
    with ctx:
        def sb(name, shape, dt=F32):
            return ctx.enter_context(nc.sbuf_tensor(name, shape, dt))

        def sem(name):
            return ctx.enter_context(nc.semaphore(name))

        scratch = nc.dram_tensor("scratch", [B, D, S], F32, kind="Internal").ap()

        xr = sb("xr", [P, HALVES, KC, HT])
        x_hi = sb("x_hi", [P, HALVES, KC, HT], F32R)
        x_lo = sb("x_lo", [P, HALVES, KC, HT], F32R)
        w = sb("w", [P, KC, D])
        w_hi = sb("w_hi", [P, KC, D], F32R)
        w_lo = sb("w_lo", [P, KC, D], F32R)
        add_rows = sb("add_rows", [LO_ROWS + NROWS, D])
        add_hl = sb("add_hl", [LO_ROWS + NROWS, D], F32R)
        ind = sb("ind", [LO_ROWS + NROWS, GT], F32R)
        con = sb("con", [P, NCONST])
        wq_sb = sb("wq_sb", [P, DC, D])
        wk_sb = sb("wk_sb", [P, DC, D])
        wv_sb = sb("wv_sb", [P, DC, D])
        wo_sb = sb("wo_sb", [P, DC, D])
        w1 = sb("w1", [P, DC, HID])
        w1_hi = sb("w1_hi", [P, DC, HID], F32R)
        w1_lo = sb("w1_lo", [P, DC, HID], F32R)
        w2 = sb("w2", [P, HC, D])
        w2_hi = sb("w2_hi", [P, HC, D], F32R)
        w2_lo = sb("w2_lo", [P, HC, D], F32R)
        b1_sb = sb("b1_sb", [P, HC])
        b2_sb = sb("b2_sb", [P, DC])
        scale_sb = sb("scale_sb", [P, 1])
        warm = sb("warm", [1, 2])
        warm_in = sb("warm_in", [P, P])
        expo = sb("expo", [GT, 1])
        h = sb("h", [GT, NG, D])
        xn = sb("xn", [GT, NG, D])
        stats = sb("stats", [GT, 4, GH, 6])
        mv = sb("mv", [GT, 4, GH, 2])
        ve = sb("ve", [GT, 4, GH])
        rstd = sb("rstd", [GT, 4, GH])
        amat = sb("amat", [P, DC, D])
        xT = sb("xT", [P, HALVES, DC, HT])
        tT = sb("tT", [P, HALVES, DC, HT])
        v = sb("v", [GT, NG, D])
        sc = sb("sc", [GT, NG, GT])
        pr = sb("pr", [GT, NG, GT])
        negmax = sb("negmax", [GT, NG])
        rsum = sb("rsum", [GT, NG])
        rinv = sb("rinv", [GT, NG])
        pT = sb("pT", [GT, NG, GT])
        oT = sb("oT", [P, HALVES, HB, DC, S])
        o2T = sb("o2T", [P, HALVES, DC, HT])
        h2 = sb("h2", [GT, NG, D])
        h2T = xT
        x2T = w[:, :, :].rearrange("p k d -> p (k d)")[:, 0:HALVES * DC * HT].rearrange(
            "p (h c t) -> p h c t", h=HALVES, c=DC)
        x2_hi = sb("x2_hi", [P, HALVES, DC, HT], F32R)
        x2_lo = sb("x2_lo", [P, HALVES, DC, HT], F32R)
        p_hi = sb("p_hi", [P, HT], F32R)
        p_part = sb("p_part", [P, HT])
        pm = sb("pm", [P, HALVES, HT], F32R)
        ev_raw = sb("ev_raw", [P, D])
        ev_hi = sb("ev_hi", [P, D], F32R)
        ev = sb("ev", [P, HALVES, D], F32R)
        e4 = sb("e4", [P, HALVES, D])
        gm = sb("gm", [P, HALVES, HT])
        xT_hi, xT_lo = x2_hi, x2_lo
        wv_hi = pm[:, :, :].rearrange("p h t -> p (h t)")[:, 0:DC * D].rearrange("p (c d) -> p c d", c=DC)
        wv_lo = ev
        even1 = sb("even1", [P, DC, P])
        odd1_hi = sb("odd1_hi", [P, DC, P], F32R)
        odd1_lo = sb("odd1_lo", [P, DC, P], F32R)
        even2 = sb("even2", [P, HALVES, DC, P])
        odd2 = sb("odd2", [P, HALVES, DC, RANK * HB])
        outT = tT
        xr_flat = xr[:, :, :, :].rearrange("p h k t -> p (h k t)")
        xh_flat = x_hi[:, :, :, :].rearrange("p h k t -> p (h k t)")
        o2 = [flat[:, HC * HT:HC * HT + len(BLOCKS) * D].rearrange("p (o d) -> p o d", d=D)
              for flat in (xr_flat, xh_flat.bitcast(F32))]
        gr = xr_flat[:, 0:HC * HT].rearrange("p (k t) -> p k t", k=HC)
        g_hi = xh_flat[:, 0:HC * HT].rearrange("p (k t) -> p k t", k=HC)
        g_lo = x_lo[:, :, :, :].rearrange("p h k t -> p (h k t)")[:, 0:HC * HT].rearrange("p (k t) -> p k t", k=HC)

        bank = [ctx.enter_context(nc.psum_tensor(f"bank{i}", [P, BANK], F32)) for i in range(8)]

        def tok_bank(g):
            return bank[g % GH]

        def xT_bank(half, c):
            return bank[((3, 4), (1, 2))[half][c]]

        def t_bank(half, c):
            return bank[((5, 6), (3, 4))[half][c]]

        def v_bank(g):
            return bank[(7, 0, 6, 5, 0, 1)[g]]

        def score_bank(g):
            return bank[(3, 4, 5, 1, 2, 6)[g]]

        pT_bank = score_bank

        def oT_bank(g):
            return bank[(7, 0, 6, 5, 3, 4)[g]]

        def o2T_bank(half, c):
            return bank[((3, 4), (2, 6))[half][c]]

        def y_bank(g):
            return bank[(0, 7, 5, 2, 6, 7)[g]]

        def hid_bank(half, k):
            n = HC * half + k
            return bank[(1, 3, 4, 5)[n if n < 4 else (n - 5) % 4] if n != 4 else 0]

        def x2T_bank(half, c):
            return bank[((2, 6), (0, 7))[half][c]]

        end_bank = (bank[2], bank[6])
        even_bank, odd_bank = bank[0], bank[7]

        ld_w = [sem(f"ld_tok_w{i}") for i in range(PIECES)]
        ld_x = [sem(f"ld_x{i}") for i in range(HALVES * PIECES)]
        ld_w0 = [sem(f"ld_first_w{k}") for k in range(PK)]
        ld_x0 = [sem(f"ld_first_x{k}") for k in range(PK)]
        ld_rows, ld_con, ld_qk, ld_wv, ld_wo = sem("ld_rows"), sem("ld_con"), sem("ld_qk"), sem("ld_wv"), sem("ld_wo")
        ld_w1, ld_w2, ld_vec = sem("ld_hid_w"), sem("ld_out_w"), sem("ld_vec")
        st_o = [sem(f"st_o{i}") for i in range(HALVES)]
        ld_o = [sem(f"ld_o{i}") for i in range(HALVES)]
        st_out = sem("st_out")
        whi_done, wlo_done, xhi_done, xlo_done = sem("whi_done"), sem("wlo_done"), sem("xhi_done"), sem("xlo_done")
        rows_done, wvhi_done, wvlo_done, xThi_ready, xTlo_ready, w1hi_done, w1lo_done, w2hi_done, w2lo_done = (
            sem("rows_done"), sem("wvhi_done"), sem("wvlo_done"), sem("xThi_ready"), sem("xTlo_ready"), sem("w1hi_done"), sem("w1lo_done"), sem("w2hi_done"), sem("w2lo_done"))
        pe_tok, pe_amat, pe_xT, pe_T, pe_v, pe_s, pe_pT, pe_oT, pe_o2T, pe_y = (
            sem(n) for n in ("pe_tok", "pe_amat", "pe_xT", "pe_T", "pe_v", "pe_s", "pe_pT", "pe_oT", "pe_o2T", "pe_y"))
        pe_x2T, pe_h2T, pe_p, pe_ev, pe_e4, pe_f1, pe_g, pe_out, pe_f2 = (
            sem(n) for n in ("pe_x2T", "pe_h2T", "pe_p", "pe_ev", "pe_e4", "pe_f1", "pe_g", "pe_out", "pe_f2"))
        h_ready, var_ready, rstd_ready, xn_ready, amat_ready, xT_first, xT_second, tT_ready, v_ready = (
            sem(n) for n in ("h_ready", "var_ready", "rstd_ready", "xn_ready", "amat_ready", "xT_first", "xT_second",
                             "tT_ready", "v_ready"))
        sc_ready, exp_ready, pr_ready, pT_ready, oT_ready, o2T_ready, h2_ready = (
            sem(n) for n in ("sc_ready", "exp_ready", "pr_ready", "pT_ready", "oT_ready", "o2T_ready", "h2_ready"))
        x2T_first, x2T_second, x2hi_first, x2hi_second, x2lo_ready, h2T_ready, phi_ready = (
            sem(n) for n in ("x2T_first", "x2T_second", "x2hi_first", "x2hi_second", "x2lo_ready", "h2T_ready", "phi_ready"))
        pm_ready, ev_ready, odd1_ready, even1_ready, even2_ready, odd2_ready, e4_ready = (
            sem(n) for n in ("pm_ready", "ev_ready", "odd1_ready", "even1_ready", "even2_ready", "odd2_ready", "e4_ready"))
        gelu_ready, ghi_done, gs_ready, gm_ready, out_ready = (
            sem(n) for n in ("gelu_ready", "ghi_done", "gs_ready", "gm_ready", "out_ready"))
        init_done, dve_chain, warm_ready = sem("init_done"), sem("dve_chain"), sem("warm_ready")

        def factors(half, first, c, part=x2T):
            return part[:, half, c, :].rearrange("p (b s) -> p s b", s=S)[:, first:first + 2 * RANK - 1:2, :]

        def inner(t):
            return t.unsqueeze(2).to_broadcast([P, RANK, 4, HB])

        def outer(t):
            return t.unsqueeze(1).to_broadcast([P, RANK, RANK, HB])

        def four(t):
            return t.rearrange("p (i r b) -> p i r b", i=RANK, b=HB)

        block = ctx.enter_context(nc.Block())

        @block.sync
        def _(sync):
            for k in range(PK):
                sync.dma_start(w[:, k, :], w_t[:, k, :]).then_inc(ld_w0[k], 16)
                sync.dma_start(xr[:, 0, k, :], x_t[0, :, k, :]).then_inc(ld_x0[k], 16)
            for i in range(1, PIECES):
                k = slice(PK * i, PK * (i + 1))
                sync.dma_start(w[:, k, :], w_t[:, k, :]).then_inc(ld_w[i], 16)
                sync.dma_start(xr[:, 0, k, :], x_t[0, :, k, :]).then_inc(ld_x[i], 16)
            sync.dma_start(con[:, :], consts).then_inc(ld_con, 16)
            sync.dma_start(add_rows[0:NROWS, :], rows).then_inc(ld_rows, 16)
            sync.dma_start(add_rows[LO_ROWS:LO_ROWS + NROWS, :], rows).then_inc(ld_rows, 16)
            sync.dma_start(wq_sb[:, :, :], wq).then_inc(ld_qk, 16)
            sync.dma_start(wk_sb[:, :, :], wk).then_inc(ld_qk, 16)
            for i in range(PIECES):
                k = slice(PK * i, PK * (i + 1))
                sync.dma_start(xr[:, 1, k, :], x_t[1, :, k, :]).then_inc(ld_x[PIECES + i], 16)
            sync.dma_start(wv_sb[:, :, :], wv_t).then_inc(ld_wv, 16)
            sync.dma_start(w1[:, :, :], w1_t).then_inc(ld_w1, 16)
            sync.dma_start(wo_sb[:, :, :], wo_t).then_inc(ld_wo, 16)
            sync.dma_start(w2[:, :, :], w2_t).then_inc(ld_w2, 16)
            sync.dma_start(b1_sb[:, :], b1_t).then_inc(ld_vec, 16)
            sync.dma_start(b2_sb[:, :], b2_t).then_inc(ld_vec, 16)
            sync.dma_start(scale_sb[:, :], scale.to_broadcast([P, 1])).then_inc(ld_vec, 16)
            for half in range(HALVES):
                for n, (b0, b1) in enumerate(((0, sum(GROUP_IMAGES[:2])), (sum(GROUP_IMAGES[:2]), HB))):
                    sync.wait_ge(oT_ready, GH * half + n + 2)
                    sync.dma_start(scratch[HB * half + b0:HB * half + b1, :, :]
                                   .rearrange("b (c p) q -> p (b c) q", c=DC),
                                   oT[:, half, b0:b1, :, :].rearrange("p b c q -> p (b c) q")).then_inc(st_o[half], 16)
                sync.wait_ge(st_o[half], 16 * 2)
                back = scratch[HB * half:HB * (half + 1), :, :].rearrange("b e q -> (b e q)")
                sync.dma_start(o2[half][:, 0:2, :], back[0:2 * P * D].rearrange("(o r d) -> r o d", o=2, d=D))\
                    .then_inc(ld_o[half], 16)
                sync.dma_start(o2[half][0:BLOCKS[2], 2, :], back[2 * P * D:HT * D].rearrange("(r d) -> r d", d=D))\
                    .then_inc(ld_o[half], 16)
            for half in range(HALVES):
                for c in range(DC):
                    sync.wait_ge(out_ready, half * DC + c + 1)
                    sync.dma_start(out_t[c, :, half * HT:(half + 1) * HT], outT[:, half, c, :]).then_inc(st_out, 16)
            sync.wait_ge(st_out, 16 * HALVES * DC)

        @block.gpsimd
        def _(pool):
            nc.gpsimd.memset(expo[:, :], -0.5).then_inc(init_done, 1)
            nc.gpsimd.memset(warm_in[:, :], 0.0).then_inc(warm_ready, 1)
            pool.wait_ge(init_done, 1)

            def powers(n):
                for i in range(GH):
                    t = span(i)[1]
                    pool.wait_ge(var_ready, GH * n + i + 1)
                    nc.gpsimd.tensor_tensor(rstd[0:t, n, i:i + 1], ve[0:t, n, i:i + 1], expo[0:t, 0:1],
                                            ALU.pow).then_inc(rstd_ready, 1)

            for n in range(3):
                powers(n)

            def second_factors(half):
                pool.wait_ge(x2T_first, half + 1)
                pool.wait_ge(x2T_second, half + 1)
                for c in range(DC):
                    nc.gpsimd.tensor_copy(four(even2[:, half, c, :]), outer(factors(half, 9, c))).then_inc(even2_ready, 1)
                for c in range(DC):
                    nc.gpsimd.tensor_copy(odd2[:, half, c, :].rearrange("p (i b) -> p i b", i=RANK),
                                          factors(half, 10, c)).then_inc(odd2_ready, 1)

            second_factors(0)
            powers(3)
            second_factors(1)

        @block.scalar
        def _(act):
            act.wait_ge(init_done, 1)
            nc.scalar.activation(warm[0:1, 0:1], expo[0:1, 0:1], ACT.Exp)

            def x_high(i):
                act.wait_ge(ld_x[i], 16)
                half, k = i // PIECES, slice(PK * (i % PIECES), PK * (i % PIECES + 1))
                nc.scalar.copy(x_hi[:, half, k, :], xr[:, half, k, :]).then_inc(xhi_done, 1)

            def w_high(i):
                for landed in (ld_w0 if i == 0 else ld_w[i:i + 1]):
                    act.wait_ge(landed, 16)
                k = slice(PK * i, PK * (i + 1))
                nc.scalar.copy(w_hi[:, k, :], w[:, k, :]).then_inc(whi_done, 1)

            def h_rows(g):
                n = span(g)[1]
                act.wait_ge(pe_tok, g + 1)
                nc.scalar.copy(h[0:n, g, :], tok_bank(g)[0:n, 0:D]).then_inc(h_ready, 1)

            def move_xT(half):
                act.wait_ge(pe_xT, DC * half + 1)
                nc.scalar.copy(xT[:, half, 0, :], xT_bank(half, 0)[:, 0:HT]).then_inc(xT_first, 1)

            def wv_high():
                act.wait_ge(ld_wv, 16)
                nc.scalar.copy(wv_hi, wv_sb[:, :, :]).then_inc(wvhi_done, 1)

            def xT_high(half):
                act.wait_ge(xT_first, half + 1)
                act.wait_ge(xT_second, half + 1)
                nc.scalar.copy(xT_hi[:, half, :, :], xT[:, half, :, :]).then_inc(xThi_ready, 1)

            def move_v(g):
                n = span(g)[1]
                act.wait_ge(pe_v, g + 1)
                nc.scalar.copy(v[0:n, g, :], v_bank(g)[0:n, 0:D]).then_inc(v_ready, 1)

            def exps(g):
                n = span(g)[1]
                act.wait_ge(sc_ready, g + 1)
                nc.scalar.activation(pr[0:n, g, 0:n], sc[0:n, g, 0:n], ACT.Exp, bias=negmax[0:n, g:g + 1],
                                     scale=-1.0, accum_out=rsum[0:n, g:g + 1]).then_inc(exp_ready, 1)

            def move_oT(g):
                b0, nb = images_of(g)
                act.wait_ge(pe_oT, g + 1)
                nc.scalar.copy(oT[:, g // GH, b0:b0 + nb, :, :], oT_bank(g)[:, 0:DC * nb * S]
                               .rearrange("p (c b q) -> p b c q", c=DC, b=nb))\
                    .then_inc(oT_ready, 1)

            def move_o2T(half, c):
                act.wait_ge(pe_o2T, DC * half + c + 1)
                nc.scalar.copy(o2T[:, half, c, :], o2T_bank(half, c)[:, 0:HT]).then_inc(o2T_ready, 1)

            def move_x2T(half):
                act.wait_ge(pe_x2T, DC * half + 1)
                nc.scalar.copy(x2_hi[:, half, 0, :], x2T_bank(half, 0)[:, 0:HT]).then_inc(x2hi_first, 1)
                nc.scalar.copy(x2T[:, half, 0, :], x2T_bank(half, 0)[:, 0:HT]).then_inc(x2T_first, 1)

            def first_factors(half):
                act.wait_ge(x2T_first, half + 1)
                act.wait_ge(x2T_second, half + 1)
                if half:
                    act.wait_ge(pe_p, half)
                    act.wait_ge(pe_ev, half)
                for c in range(DC):
                    nc.scalar.copy(four(even1[:, c, :]), inner(factors(half, 1, c))).then_inc(even1_ready, 1)
                for c in range(DC):
                    nc.scalar.copy(four(odd1_hi[:, c, :]), inner(factors(half, 2, c, x2_hi))).then_inc(odd1_ready, 1)
                for c in range(DC):
                    act.wait_ge(x2lo_ready, DC * half + c + 1)
                    nc.scalar.copy(four(odd1_lo[:, c, :]), inner(factors(half, 2, c, x2_lo))).then_inc(odd1_ready, 1)

            def move_h2T(half):
                for c in range(DC):
                    act.wait_ge(pe_h2T, DC * half + c + 1)
                    nc.scalar.copy(h2T[:, half, c, :], end_bank[c][:, 0:HT]).then_inc(h2T_ready, 1)

            def p_high(half):
                act.wait_ge(pe_p, half + 1)
                if half:
                    act.wait_ge(pm_ready, half)
                nc.scalar.copy(p_hi[:, :], odd_bank[:, 0:HT]).then_inc(phi_ready, 1)

            def gelus(half, ks):
                for k in ks:
                    act.wait_ge(pe_f1, HC * half + k + 1)
                    if half:
                        act.wait_ge(pe_g, 1)
                    nc.scalar.activation(gr[:, k, :], hid_bank(half, k)[:, 0:HT], ACT.Gelu,
                                         bias=b1_sb[:, k:k + 1]).then_inc(gelu_ready, 1)

            def g_high(half, ks):
                for k in ks:
                    act.wait_ge(gelu_ready, HC * half + k + 1)
                    if half:
                        act.wait_ge(pe_out, 1)
                    nc.scalar.copy(g_hi[:, k, :], gr[:, k, :]).then_inc(ghi_done, 1)

            def w1_high(c):
                act.wait_ge(ld_w1, 16)
                nc.scalar.copy(w1_hi[:, c, :], w1[:, c, :]).then_inc(w1hi_done, 1)

            def w2_high(c):
                act.wait_ge(ld_w2, 16)
                k = slice(4 * c, 4 * c + 4)
                nc.scalar.copy(w2_hi[:, k, :], w2[:, k, :]).then_inc(w2hi_done, 1)

            for i in range(1, PIECES):
                w_high(i)
                x_high(i)
            w_high(0)
            x_high(PIECES)
            h_rows(0)
            h_rows(1)
            x_high(PIECES + 1)
            h_rows(2)
            x_high(PIECES + 2)
            act.wait_ge(pe_amat, 1)
            nc.scalar.mul(amat[:, :, :].rearrange("p c d -> p (c d)"), bank[5][:, :], -0.25).then_inc(amat_ready, 1)
            wv_high()
            move_xT(0)
            xT_high(0)
            h_rows(3)
            w1_high(0)
            for g in range(GH):
                exps(g)
            move_v(0)
            w1_high(1)
            h_rows(4)
            move_v(1)
            w2_high(0)
            w2_high(1)
            h_rows(5)
            move_oT(0)
            move_v(2)
            move_oT(1)
            move_xT(1)
            move_oT(2)
            xT_high(1)
            move_v(3)
            for g in range(GH, NG):
                exps(g)
            move_v(4)
            move_o2T(0, 0)
            move_oT(3)
            nc.scalar.activation(warm[0:1, 1:2], expo[0:1, 0:1], ACT.Gelu)
            move_v(5)
            move_oT(4)
            move_x2T(0)
            move_oT(5)
            first_factors(0)
            p_high(0)
            act.wait_ge(ld_vec, 48)
            gelus(0, range(3))
            move_o2T(1, 0)
            gelus(0, range(3, 5))
            g_high(0, range(3))
            gelus(0, range(5, 6))
            g_high(0, range(3, 5))
            move_h2T(0)
            gelus(0, range(6, 7))
            move_h2T(1)
            g_high(0, range(5, 7))
            gelus(0, range(7, HC))
            move_x2T(1)
            first_factors(1)
            g_high(0, range(7, HC))
            p_high(1)
            for k in range(HC):
                gelus(1, range(k, k + 1))
                g_high(1, range(k, k + 1))

        @block.vector
        def _(dve):
            chained = [0]

            def then(instruction):
                chained[0] += 1
                instruction.then_inc(dve_chain, 1)
                dve.wait_ge(dve_chain, chained[0])

            def w_low(i):
                k = slice(PK * i, PK * (i + 1))
                for landed in (ld_w0 if i == 0 else ld_w[i:i + 1]):
                    dve.wait_ge(landed, 16)
                dve.wait_ge(whi_done, i if i else PIECES)
                nc.vector.tensor_tensor(w_lo[:, k, :], w[:, k, :], w_hi[:, k, :], ALU.subtract).then_inc(wlo_done, 1)

            def x_low(i):
                half, k = i // PIECES, slice(PK * (i % PIECES), PK * (i % PIECES + 1))
                dve.wait_ge(ld_x[i], 16)
                dve.wait_ge(xhi_done, i)
                nc.vector.tensor_tensor(x_lo[:, half, k, :], xr[:, half, k, :], x_hi[:, half, k, :],
                                        ALU.subtract).then_inc(xlo_done, 1)

            def norm_begin(n, rows_, ready, g):
                t, i = span(g)[1], g % GH
                dve.wait_ge(ready, g + 1)
                nc.vector.bn_stats(stats[0:t, n, i, :], rows_[0:t, g, :]).then_inc(dve_chain, 1)
                chained[0] += 1
                return chained[0]

            def norm_end(n, g, stats_written):
                t, i = span(g)[1], g % GH
                dve.wait_ge(dve_chain, stats_written)
                then(nc.vector.bn_aggr(mv[0:t, n, i, :], stats[0:t, n, i, :]))
                nc.vector.tensor_scalar(ve[0:t, n, i:i + 1], mv[0:t, n, i, 1:2], EPS, None, ALU.add)\
                    .then_inc(var_ready, 1)

            def norm_stats(n, rows_, ready, g):
                norm_end(n, g, norm_begin(n, rows_, ready, g))

            def norm_rows(n, rows_, g):
                t, i = span(g)[1], g % GH
                dve.wait_ge(rstd_ready, GH * n + i + 1)
                if n >= HALVES:
                    dve.wait_ge(pe_xT, DC * (n - 1))
                nc.vector.tensor_scalar(xn[0:t, g, :], rows_[0:t, g, :], mv[0:t, n, i, 0:1], rstd[0:t, n, i:i + 1],
                                        ALU.subtract, ALU.mult).then_inc(xn_ready, 1)

            def move_xT(half):
                dve.wait_ge(pe_xT, DC * half + DC)
                nc.vector.tensor_copy(xT[:, half, 1, :], xT_bank(half, 1)[:, 0:HT]).then_inc(xT_second, 1)

            def move_o2T(half, c):
                dve.wait_ge(pe_o2T, DC * half + c + 1)
                nc.vector.tensor_copy(o2T[:, half, c, :], o2T_bank(half, c)[:, 0:HT]).then_inc(o2T_ready, 1)

            def move_T(half):
                for c in range(DC):
                    dve.wait_ge(pe_T, DC * half + c + 1)
                    nc.vector.tensor_copy(tT[:, half, c, :], t_bank(half, c)[:, 0:HT]).then_inc(tT_ready, 1)

            def masked_max(g):
                nb = images_of(g)[1]
                n = nb * S
                dve.wait_ge(pe_s, g + 1)
                nc.vector.tensor_tensor_reduce(
                    out=sc[0:n, g, 0:n].rearrange("p (b k) -> p b k", k=S),
                    in0=score_bank(g)[0:n, 0:n].rearrange("p (b k) -> p b k", k=S),
                    in1=con[0:n, C_ATT:C_ATT + nb].unsqueeze(2).to_broadcast([n, nb, S]),
                    scale=1.0, scalar=3e38, op0=ALU.add, op1=ALU.min,
                    accum_out=negmax[0:n, g:g + 1]).then_inc(sc_ready, 1)

            def softmax_end(g):
                n = span(g)[1]
                dve.wait_ge(exp_ready, g + 1)
                then(nc.vector.reciprocal(rinv[0:n, g:g + 1], rsum[0:n, g:g + 1]))
                nc.vector.tensor_scalar(pr[0:n, g, 0:n], pr[0:n, g, 0:n], rinv[0:n, g:g + 1], None,
                                        ALU.mult).then_inc(pr_ready, 1)

            def move_pT(g):
                n = span(g)[1]
                dve.wait_ge(pe_pT, g + 1)
                nc.vector.tensor_copy(pT[0:n, g, 0:n], pT_bank(g)[0:n, 0:n]).then_inc(pT_ready, 1)

            def residual(g):
                n = span(g)[1]
                dve.wait_ge(pe_y, g + 1)
                nc.vector.tensor_tensor(h2[0:n, g, :], y_bank(g)[0:n, 0:D], h[0:n, g, :], ALU.add)\
                    .then_inc(h2_ready, 1)

            def second_norm(half):
                begun = None
                for g in range(GH * half, GH * (half + 1)):
                    residual(g)
                    if begun is not None:
                        norm_end(2 + half, g - 1, begun)
                    begun = norm_begin(2 + half, h2, h2_ready, g)
                norm_rows(2 + half, h2, g - 2)
                norm_end(2 + half, g, begun)
                norm_rows(2 + half, h2, g - 1)
                norm_rows(2 + half, h2, g)

            def second_T(half):
                dve.wait_ge(pe_x2T, DC * half + DC)
                nc.vector.tensor_copy(x2_hi[:, half, 1, :], x2T_bank(half, 1)[:, 0:HT]).then_inc(x2hi_second, 1)
                nc.vector.tensor_copy(x2T[:, half, 1, :], x2T_bank(half, 1)[:, 0:HT]).then_inc(x2T_second, 1)

            def x2_low(half):
                for c in range(DC):
                    dve.wait_ge((x2T_first, x2T_second)[c], half + 1)
                    nc.vector.tensor_tensor(x2_lo[:, half, c, :], x2T[:, half, c, :], x2_hi[:, half, c, :],
                                            ALU.subtract).then_inc(x2lo_ready, 1)

            def factors_ready(half):
                dve.wait_ge(pe_ev, half + 1)
                then(nc.vector.tensor_scalar(ev_raw[:, :], even_bank[:, 0:D], scale_sb[:, 0:1], None, ALU.mult))
                then(nc.vector.tensor_copy(ev_hi[:, :], ev_raw[:, :]))
                nc.vector.scalar_tensor_tensor(out=ev[:, half, :], in0=ev_raw[:, :],
                                               scalar=con[:, C_SE:C_SE + 1], in1=ev_hi[:, :],
                                               op0=ALU.mult, op1=ALU.subtract).then_inc(ev_ready, 1)

            def second_even(half):
                dve.wait_ge(pe_e4, half + 1)
                for j in range(RANK):
                    rows_ = slice(32 * j, 32 * (j + 1))
                    last = nc.vector.tensor_tensor(
                        e4[rows_, half, :].rearrange("p (i o) -> p i o", i=RANK),
                        even_bank[rows_, j:D:RANK].unsqueeze(1).to_broadcast([32, RANK, D // RANK]),
                        con[rows_, C_IM:C_IM + RANK].unsqueeze(2).to_broadcast([32, RANK, D // RANK]), ALU.mult)
                last.then_inc(e4_ready, 1)

            def projection_parts(half):
                dve.wait_ge(phi_ready, half + 1)
                then(nc.vector.scalar_tensor_tensor(out=p_part[:, :], in0=odd_bank[:, 0:HT],
                                                    scalar=con[:, C_SP:C_SP + 1], in1=p_hi[:, :],
                                                    op0=ALU.mult, op1=ALU.subtract))
                nc.vector.tensor_tensor(
                    pm[:, half, :].rearrange("p (b s) -> p b s", s=S),
                    p_part[:, :].rearrange("p (b s) -> p b s", s=S),
                    con[:, C_PM:C_PM + HB].unsqueeze(2).to_broadcast([P, HB, S]), ALU.mult).then_inc(pm_ready, 1)

            def g_low(half, ks):
                for k in ks:
                    dve.wait_ge(ghi_done, HC * half + k + 1)
                    nc.vector.tensor_tensor(g_lo[:, k, :], gr[:, k, :], g_hi[:, k, :], ALU.subtract)\
                        .then_inc(gs_ready, 1)

            def mask_g(half):
                dve.wait_ge(pe_g, half + 1)
                nc.vector.scalar_tensor_tensor(
                    out=gm[:, half, :].rearrange("p (b s) -> p b s", s=S),
                    in0=odd_bank[:, 0:HT].rearrange("p (b s) -> p b s", s=S), scalar=scale_sb[:, 0:1],
                    in1=con[:, C_GM:C_GM + HB].unsqueeze(2).to_broadcast([P, HB, S]),
                    op0=ALU.mult, op1=ALU.mult).then_inc(gm_ready, 1)

            def finish(half):
                for c in range(DC):
                    dve.wait_ge(pe_f2, DC * half + c + 1)
                    dve.wait_ge(h2T_ready, DC * half + c + 1)
                    nc.vector.scalar_tensor_tensor(out=outT[:, half, c, :], in0=end_bank[c][:, 0:HT],
                                                   scalar=b2_sb[:, c:c + 1], in1=h2T[:, half, c, :],
                                                   op0=ALU.add, op1=ALU.add).then_inc(out_ready, 1)

            def wv_low():
                dve.wait_ge(wvhi_done, 1)
                nc.vector.tensor_tensor(wv_lo[:, :, :], wv_sb[:, :, :], wv_hi, ALU.subtract).then_inc(wvlo_done, 1)

            def xT_low(half):
                dve.wait_ge(xThi_ready, half + 1)
                nc.vector.tensor_tensor(xT_lo[:, half, :, :], xT[:, half, :, :], xT_hi[:, half, :, :], ALU.subtract)\
                    .then_inc(xTlo_ready, 1)

            def w1_low(c):
                dve.wait_ge(w1hi_done, c + 1)
                nc.vector.tensor_tensor(w1_lo[:, c, :], w1[:, c, :], w1_hi[:, c, :], ALU.subtract).then_inc(w1lo_done, 1)

            def w2_low(c):
                k = slice(4 * c, 4 * c + 4)
                dve.wait_ge(w2hi_done, c + 1)
                nc.vector.tensor_tensor(w2_lo[:, k, :], w2[:, k, :], w2_hi[:, k, :], ALU.subtract).then_inc(w2lo_done, 1)

            then(nc.vector.memset(add_hl[:, :].bitcast(F32), 0.0))
            for i in range(1, PIECES):
                w_low(i)
                x_low(i)
            dve.wait_ge(ld_con, 16)
            nc.vector.tensor_copy(ind[:, :], con[0:LO_ROWS + NROWS, C_IND:C_IND + GT])
            dve.wait_ge(ld_rows, 32)
            then(nc.vector.tensor_copy(add_hl[LO_ROWS:LO_ROWS + NROWS, :], add_rows[LO_ROWS:LO_ROWS + NROWS, :]))
            nc.vector.tensor_copy(add_hl[0:NROWS, :], add_rows[0:NROWS, :])
            nc.vector.tensor_tensor(add_hl[LO_ROWS:LO_ROWS + NROWS, :], add_rows[LO_ROWS:LO_ROWS + NROWS, :],
                                    add_hl[LO_ROWS:LO_ROWS + NROWS, :], ALU.subtract).then_inc(rows_done, 1)
            w_low(0)
            x_low(PIECES)
            begun = [norm_begin(0, h, h_ready, g) for g in range(2)]
            norm_end(0, 0, begun[0])
            norm_end(0, 1, begun[1])
            norm_stats(0, h, h_ready, 2)
            for g in range(GH):
                norm_rows(0, h, g)
            move_xT(0)
            x_low(PIECES + 1)
            x_low(PIECES + 2)
            move_T(0)
            wv_low()
            xT_low(0)
            norm_stats(1, h, h_ready, 3)
            for g in range(GH):
                masked_max(g)
            norm_rows(1, h, 3)
            w1_low(0)
            for g in range(GH):
                softmax_end(g)
            norm_stats(1, h, h_ready, 4)
            for g in range(GH):
                move_pT(g)
            norm_rows(1, h, 4)
            w1_low(1)
            norm_stats(1, h, h_ready, 5)
            norm_rows(1, h, 5)
            move_xT(1)
            w2_low(0)
            move_T(1)
            xT_low(1)
            for g in range(GH, NG):
                masked_max(g)
            for g in range(GH, NG):
                softmax_end(g)
            for g in range(GH, NG):
                move_pT(g)
            move_o2T(0, 1)
            w2_low(1)
            second_norm(0)
            second_T(0)
            x2_low(0)
            dve.wait_ge(ld_vec, 48)
            factors_ready(0)
            projection_parts(0)
            move_o2T(1, 1)
            second_norm(1)
            g_low(0, range(3))
            second_T(1)
            g_low(0, range(3, 4))
            x2_low(1)
            g_low(0, range(4, HC))
            factors_ready(1)
            projection_parts(1)
            second_even(0)
            mask_g(0)
            g_low(1, range(1))
            finish(0)
            g_low(1, range(1, HC))
            second_even(1)
            mask_g(1)
            finish(1)

        @block.tensor
        def _(pe):
            ident = con[:, C_ID:C_ID + P]

            def three(out, s_hi, s_lo, m_hi, m_lo, start, stop):
                nc.tensor.matmul(out, s_lo, m_hi, start=start, stop=False)
                nc.tensor.matmul(out, s_hi, m_lo, start=False, stop=False)
                return nc.tensor.matmul(out, s_hi, m_hi, start=False, stop=stop)

            def tok_piece(g, i):
                half, (cols, n) = g // GH, span(g)
                for k in range(PK * i, PK * (i + 1)):
                    three(tok_bank(g)[0:n, 0:D], x_hi[:, half, k, cols], x_lo[:, half, k, cols],
                          w_hi[:, k, :], w_lo[:, k, :], k == 0, False)

            def tok_rows(g):
                n = span(g)[1]
                pe.wait_ge(rows_done, 1)
                nc.tensor.matmul(tok_bank(g)[0:n, 0:D], ind[:, 0:n], add_hl[:, :], start=False, stop=True)\
                    .then_inc(pe_tok, 1)

            def tok_group(g, pieces=range(PIECES)):
                pe.wait_ge(h_ready, g - GH + 1)
                pe.wait_ge(wlo_done, PIECES)
                for i in pieces:
                    pe.wait_ge(xlo_done, PIECES + i)
                    tok_piece(g, i)
                if PIECES - 1 in pieces:
                    tok_rows(g)

            def to_T(rows_, half, out, done, ready=None, before=0):
                for g in range(half * GH, (half + 1) * GH):
                    cols, n = span(g)
                    if ready is not None:
                        pe.wait_ge(ready, before + g + 1)
                    for c in range(DC):
                        last = nc.tensor.transpose(out[c][:, cols], rows_[0:n, g, P * c:P * (c + 1)], ident[0:n, 0:n])
                        if g == (half + 1) * GH - 1:
                            last.then_inc(done, 1)

            def x_T(half):
                if half:
                    pe.wait_ge(h_ready, NG)
                to_T(xn, half, [xT_bank(half, c) for c in range(DC)], pe_xT, xn_ready)

            def t_T(half):
                pe.wait_ge(amat_ready, 1)
                if half:
                    pe.wait_ge(pT_ready, 2)
                for k in range(DC):
                    pe.wait_ge((xT_first, xT_second)[k], half + 1)
                    for c in range(DC):
                        last = nc.tensor.matmul(t_bank(half, c)[:, 0:HT], amat[:, k, P * c:P * (c + 1)],
                                                xT[:, half, k, :], start=k == 0, stop=k == DC - 1)
                        if k == DC - 1:
                            last.then_inc(pe_T, 1)

            def values(g):
                half, (cols, n) = g // GH, span(g)
                if g == GH:
                    pe.wait_ge(ld_wv, 16)
                else:
                    pe.wait_ge(wvlo_done, 1)
                    pe.wait_ge(xTlo_ready, half + 1)
                if g:
                    pe.wait_ge(*((h_ready, 4), (tT_ready, DC), (pT_ready, GH), (oT_ready, 2), (pT_ready, 4))[g - 1])
                for k in range(DC):
                    if g == GH:
                        last = nc.tensor.matmul(v_bank(g)[0:n, 0:D], xT[:, half, k, cols], wv_sb[:, k, :],
                                                start=k == 0, stop=k == DC - 1)
                        continue
                    last = three(v_bank(g)[0:n, 0:D], xT_hi[:, half, k, cols], xT_lo[:, half, k, cols],
                                 wv_hi[:, k, :], wv_lo[:, k, :], k == 0, k == DC - 1)
                last.then_inc(pe_v, 1)

            def scores(g):
                half, (cols, n) = g // GH, span(g)
                pe.wait_ge(tT_ready, DC * (half + 1))
                if half:
                    pe.wait_ge(oT_ready, GH)
                for k in range(DC):
                    last = nc.tensor.matmul(score_bank(g)[0:n, 0:n], tT[:, half, k, cols], xT[:, half, k, cols],
                                            start=k == 0, stop=k == DC - 1)
                last.then_inc(pe_s, 1)

            def attend_T(g):
                n = span(g)[1]
                pe.wait_ge(pr_ready, g + 1)
                nc.tensor.transpose(pT_bank(g)[0:n, 0:n], pr[0:n, g, 0:n], ident[0:n, 0:n]).then_inc(pe_pT, 1)

            def attend(g):
                n = span(g)[1]
                pe.wait_ge(pT_ready, g + 1)
                pe.wait_ge(v_ready, g + 1)
                pe.wait_ge(*((v_ready, 1), (v_ready, 2), (v_ready, 3), (v_ready, 4), (o2T_ready, DC), (o2T_ready, DC))[g])
                for c in range(DC):
                    last = nc.tensor.matmul(oT_bank(g)[:, c * n:(c + 1) * n], v[0:n, g, P * c:P * (c + 1)],
                                            pT[0:n, g, 0:n], start=True, stop=True)
                last.then_inc(pe_oT, 1)

            def o2_T(half):
                pe.wait_ge(*((tT_ready, DC * HALVES), (x2T_first, 1))[half])
                if half:
                    pe.wait_ge(x2T_second, 1)
                pe.wait_ge(ld_o[half], 32)
                for c in range(DC):
                    for i, n in enumerate(BLOCKS):
                        last = nc.tensor.transpose(o2T_bank(half, c)[:, P * i:P * i + n],
                                                   o2[half][0:n, i, P * c:P * (c + 1)], ident[0:n, 0:n])
                    last.then_inc(pe_o2T, 1)

            def project(g):
                half, (cols, n) = g // GH, span(g)
                pe.wait_ge(ld_wo, 16)
                pe.wait_ge(o2T_ready, DC * (half + 1))
                pe.wait_ge(*((v_ready, 5), (oT_ready, 1), (oT_ready, 4), (o2T_ready, DC * HALVES),
                             (o2T_ready, DC * HALVES), (pm_ready, 1))[g])
                for k in range(DC):
                    last = nc.tensor.matmul(y_bank(g)[0:n, 0:D], o2T[:, half, k, cols], wo_sb[:, k, :],
                                            start=k == 0, stop=k == DC - 1)
                last.then_inc(pe_y, 1)

            def x2_T(half):
                if half:
                    pe.wait_ge(gelu_ready, 5)
                    pe.wait_ge(h2_ready, NG)
                else:
                    pe.wait_ge(pT_ready, NG)
                to_T(xn, half, [x2T_bank(half, c) for c in range(DC)], pe_x2T, xn_ready, NG)

            def h2_T(half):
                if half:
                    pe.wait_ge(h2_ready, NG)
                    pe.wait_ge(h2T_ready, DC)
                else:
                    pe.wait_ge(h2_ready, 5)
                to_T(h2, half, end_bank, pe_h2T)

            def first_even_rows(half):
                pe.wait_ge(even1_ready, DC * (half + 1))
                pe.wait_ge(*((h2_ready, 1), (x2T_first, 2))[half])
                for c in range(DC):
                    last = nc.tensor.transpose(even_bank[:, P * c:P * (c + 1)], even1[:, c, :], ident)
                last.then_inc(pe_ev, 1)

            def projection(half):
                pe.wait_ge(odd1_ready, 2 * DC * (half + 1))
                pe.wait_ge(*((h2_ready, GH), (pm_ready, 1))[half])
                for c in range(DC):
                    last = three(odd_bank[:, 0:HT], odd1_hi[:, c, :], odd1_lo[:, c, :], x2_hi[:, half, c, :],
                                 x2_lo[:, half, c, :], c == 0, c == DC - 1)
                last.then_inc(pe_p, 1)

            def second_even_rows(half):
                pe.wait_ge(even2_ready, DC * (half + 1))
                pe.wait_ge(ev_ready, HALVES)
                for c in range(DC):
                    last = nc.tensor.transpose(even_bank[:, P * c:P * (c + 1)], even2[:, half, c, :], ident)
                last.then_inc(pe_e4, 1)

            def hidden_high(half, k):
                pe.wait_ge(w1lo_done, DC)
                pe.wait_ge(x2hi_first, half + 1)
                n = HC * half + k
                if n > 8:
                    pe.wait_ge(gelu_ready, n - 3)
                elif n > 4:
                    pe.wait_ge(gelu_ready, n - 4)
                elif n == 4:
                    pe.wait_ge(ev_ready, 1)
                else:
                    pe.wait_ge(*((v_ready, NG), (oT_ready, 5), (oT_ready, NG), (h2_ready, GH))[k])
                cols = slice(P * k, P * (k + 1))
                for c in range(DC):
                    if c:
                        pe.wait_ge(x2hi_second, half + 1)
                    for part in (w1_lo, w1_hi):
                        nc.tensor.matmul(hid_bank(half, k)[:, 0:HT], part[:, c, cols], x2_hi[:, half, c, :],
                                         start=c == 0 and part is w1_lo, stop=False)

            def hidden_low(half, k):
                for c in range(DC):
                    pe.wait_ge(x2lo_ready, DC * half + c + 1)
                    nc.tensor.matmul(hid_bank(half, k)[:, 0:HT], w1_hi[:, c, P * k:P * (k + 1)], x2_lo[:, half, c, :],
                                     start=False, stop=False)

            def hidden_low_rank(half, k):
                i, c = k // 2, k % 2
                pe.wait_ge(pm_ready, half + 1)
                pe.wait_ge(ev_ready, half + 1)
                nc.tensor.matmul(hid_bank(half, k)[:, 0:HT], ev[32 * i:32 * (i + 1), half, P * c:P * (c + 1)],
                                 pm[32 * i:32 * (i + 1), half, :], start=False, stop=True).then_inc(pe_f1, 1)

            def output(half, k, cs):
                pe.wait_ge(*((h2T_ready, DC * HALVES), (out_ready, DC))[half])
                pe.wait_ge(w2lo_done, k // 4 + 1)
                pe.wait_ge(gs_ready, HC * half + k + 1)
                for c in cs:
                    cols = slice(P * c, P * (c + 1))
                    last = three(end_bank[c][:, 0:HT], w2_hi[:, k, cols], w2_lo[:, k, cols], g_hi[:, k, :],
                                 g_lo[:, k, :], k == 0, False)
                return last

            def hidden_on_odd(half):
                pe.wait_ge(gelu_ready, HC * (half + 1))
                pe.wait_ge(odd2_ready, DC * (half + 1))
                pe.wait_ge(pm_ready, HALVES)
                for c in range(DC):
                    for j in range(RANK):
                        last = nc.tensor.matmul(odd_bank[32 * j:32 * (j + 1), 0:HT], odd2[:, half, c, :],
                                                gr[:, DC * j + c, :], start=c == 0, stop=c == DC - 1)
                last.then_inc(pe_g, 1)

            def output_low_rank(half, cs):
                pe.wait_ge(gm_ready, half + 1)
                pe.wait_ge(e4_ready, half + 1)
                for c in cs:
                    nc.tensor.matmul(end_bank[c][:, 0:HT], e4[:, half, P * c:P * (c + 1)], gm[:, half, :],
                                     start=False, stop=True).then_inc(pe_f2, 1)

            def hidden(half, k):
                hidden_high(half, k)
                hidden_low(half, k)
                hidden_low_rank(half, k)

            def keep_clock(products):
                for _ in range(products):
                    nc.tensor.matmul(bank[4][:, 0:P], warm_in[:, :], warm_in[:, :], start=True, stop=True)

            pe.wait_ge(warm_ready, 1)
            keep_clock(WARM)
            for k in range(PK):
                pe.wait_ge(ld_w0[k], 16)
                pe.wait_ge(ld_x0[k], 16)
                for g in range(GH):
                    cols, n = span(g)
                    nc.tensor.matmul(tok_bank(g)[0:n, 0:D], xr[:, 0, k, cols], w[:, k, :], start=k == 0, stop=False)
            for i in range(1, PIECES):
                pe.wait_ge(wlo_done, i)
                pe.wait_ge(xlo_done, i)
                for g in range(GH):
                    tok_piece(g, i)
                    if i == PIECES - 1:
                        tok_rows(g)
            pe.wait_ge(ld_qk, 32)
            pe.wait_ge(ld_con, 16)
            for c in range(DC):
                for k in range(DC):
                    last = nc.tensor.matmul(bank[5][:, D * c:D * (c + 1)], wq_sb[:, k, P * c:P * (c + 1)],
                                            wk_sb[:, k, :], start=k == 0, stop=k == DC - 1)
            last.then_inc(pe_amat, 1)
            tok_group(3, range(1))
            x_T(0)
            t_T(0)
            tok_group(3, range(1, PIECES))
            for g in range(GH):
                scores(g)
            values(0)
            tok_group(4)
            values(1)
            for g in range(GH):
                attend_T(g)
            tok_group(5)
            attend(0)
            values(2)
            attend(1)
            x_T(1)
            attend(2)
            t_T(1)
            values(3)
            for g in range(GH, NG):
                scores(g)
            values(4)
            for g in range(GH, NG):
                attend_T(g)
            o2_T(0)
            attend(3)
            for g in range(GH):
                project(g)
            values(5)
            attend(4)
            keep_clock(KEEP)
            x2_T(0)
            attend(5)
            hidden_high(0, 0)
            hidden_high(0, 1)
            first_even_rows(0)
            hidden_high(0, 2)
            projection(0)
            hidden_high(0, 3)
            for k in range(4):
                hidden_low(0, k)
            hidden_high(0, 4)
            hidden_low(0, 4)
            for k in range(5):
                hidden_low_rank(0, k)
            o2_T(1)
            hidden(0, 5)
            for g in range(GH, NG):
                project(g)
            h2_T(0)
            hidden(0, 6)
            h2_T(1)
            hidden(0, 7)
            x2_T(1)
            for k in range(4):
                output(0, k, range(DC))
            first_even_rows(1)
            projection(1)
            for k in range(4, HC):
                last = output(0, k, range(DC))
            last.then_inc(pe_out, 1)
            second_even_rows(0)
            hidden_on_odd(0)
            for k in range(4):
                hidden(1, k)
            output_low_rank(0, range(DC))
            for k in range(4, HC):
                hidden(1, k)
            for k in range(6):
                output(1, k, range(DC))
            second_even_rows(1)
            hidden_on_odd(1)
            for c in range(DC):
                output(1, 6, (c,))
                output(1, 7, (c,))
                output_low_rank(1, (c,))


def kernel(x, cls_tok, L0_tok_W, L0_tok_b, L0_tok_cls_token, L0_tok_pos_embedding, L0_attn_wq, L0_attn_wk,
           L0_attn_wv, L0_attn_wo, L0_ffn_W1, L0_ffn_b1, L0_ffn_W2, L0_ffn_b2, L0_ffn_scale):
    import concourse.bacc as bacc
    from concourse.bass_utils import run_bass_kernel_spmd

    def chunks(a):
        a = np.asarray(a)
        return np.ascontiguousarray(a.reshape(-1, P, a.shape[1]).transpose(1, 0, 2))

    n = IMG // PATCH
    patches = np.asarray(x).reshape(B, CH, n, PATCH, n, PATCH).transpose(0, 2, 4, 1, 3, 5).reshape(B, NPATCH, KD)
    tokens = np.zeros((B, S, KD), np.float32)
    tokens[:, S - NPATCH:, :] = patches
    x_t = tokens.reshape(HALVES, HT, KC, P).transpose(0, 3, 2, 1)
    rows = np.concatenate([np.asarray(cls_tok).reshape(1, D), np.asarray(L0_tok_cls_token).reshape(1, D),
                           np.asarray(L0_tok_b).reshape(1, D), np.asarray(L0_tok_pos_embedding).reshape(-1, D)])
    arrays = {
        "x_t": x_t, "w_t": chunks(np.asarray(L0_tok_W).T), "rows": rows, "consts": constants(),
        "wq": chunks(L0_attn_wq), "wk": chunks(L0_attn_wk),
        "wv_t": chunks(np.asarray(L0_attn_wv).T), "wo_t": chunks(np.asarray(L0_attn_wo).T),
        "w1_t": chunks(np.asarray(L0_ffn_W1).T), "w2_t": chunks(np.asarray(L0_ffn_W2).T),
        "b1_t": np.asarray(L0_ffn_b1).reshape(HC, P).T, "b2_t": np.asarray(L0_ffn_b2).reshape(DC, P).T,
        "scale": np.asarray(L0_ffn_scale).reshape(1, 1),
    }
    arrays = {k: np.ascontiguousarray(a) for k, a in arrays.items()}
    nc = bacc.Bacc("TRN2", target_bir_lowering=False, num_devices=1)
    args = [nc.dram_tensor(k, a.shape, mybir.dt.from_np(a.dtype), kind="ExternalInput").ap() for k, a in arrays.items()]
    out_t = nc.dram_tensor("out_t", (DC, P, B * S), F32, kind="ExternalOutput").ap()
    build(nc, *args, out_t)
    result = run_bass_kernel_spmd(nc, [arrays], core_ids=[0]).results[0]["out_t"]
    return np.ascontiguousarray(result.reshape(D, B, S).transpose(1, 2, 0))
```
